# Optimizing a Trainium2 kernel written in Bass

```python
import numpy as np
import jax
import jax.numpy as jnp

def _softmax(x, axis=-1):
    return jax.nn.softmax(x, axis=axis)

def _gelu(x):
    return jax.nn.gelu(x, approximate=True)

def _silu(x):
    return jax.nn.silu(x)

def _sigmoid(x):
    return jax.nn.sigmoid(x)

def _layernorm(x, axis=-1, eps=1e-05):
    m = jnp.mean(x, axis=axis, keepdims=True)
    v = jnp.var(x, axis=axis, keepdims=True)
    return (x - m) / jnp.sqrt(v + eps)

def _scatter_add(tgt, idx, src, axis=0):
    return tgt.at[idx].add(src)

def _segment_sum(src, seg, n):
    return jax.ops.segment_sum(src, seg, n)
kernel_name = 'mk_seq_preln_d1_jaxref_r4_b83001'

def setup_inputs(seed: int=0):
    np.random.seed(seed)
    _w = jnp.asarray

    def _L0_attn_setup():
        import math
        import jax, jax.numpy as jnp
        import numpy as np
        B, T, D = (2, 512, 512)
        NH, NKV = (32, 8)
        HD = D // NH
        key = jax.random.key(seed)
        kx, kq, kk, kv, ko = jax.random.split(key, 5)
        s = 1.0 / math.sqrt(D)
        return {'x': jax.random.normal(kx, (B, T, D), dtype=jnp.float32), 'wq': jax.random.normal(kq, (D, NH * HD), dtype=jnp.float32) * s, 'wk': jax.random.normal(kk, (D, NKV * HD), dtype=jnp.float32) * s, 'wv': jax.random.normal(kv, (D, NKV * HD), dtype=jnp.float32) * s, 'wo': jax.random.normal(ko, (NH * HD, D), dtype=jnp.float32) * s}
    _L0_attn_in = _L0_attn_setup()

    def _L0_ffn_setup():
        import jax, jax.numpy as jnp
        import numpy as np
        B, T, D = (2, 256, 512)
        E, F, K = (64, 128, 4)
        S, HS = (2, 128 * 4)
        key = jax.random.key(seed)
        ks = jax.random.split(key, 9)
        s = 0.02
        f32 = jnp.float32
        return {'x': jax.random.normal(ks[0], (B, T, D), f32), 'router_w': jax.random.normal(ks[1], (D, E), f32) * s, 'router_bias': jnp.zeros((E,), f32), 'wg': jax.random.normal(ks[2], (E, D, F), f32) * s, 'wu': jax.random.normal(ks[3], (E, D, F), f32) * s, 'wd': jax.random.normal(ks[4], (E, F, D), f32) * s, 'swg': jax.random.normal(ks[5], (S, D, HS), f32) * s, 'swu': jax.random.normal(ks[6], (S, D, HS), f32) * s, 'swd': jax.random.normal(ks[7], (S, HS, D), f32) * s}
    _L0_ffn_in = _L0_ffn_setup()
    _d = {'L0_attn_x': _L0_attn_in['x'], 'L0_attn_wq': _L0_attn_in['wq'], 'L0_attn_wk': _L0_attn_in['wk'], 'L0_attn_wv': _L0_attn_in['wv'], 'L0_attn_wo': _L0_attn_in['wo'], 'L0_ffn_router_w': _L0_ffn_in['router_w'], 'L0_ffn_router_bias': _L0_ffn_in['router_bias'], 'L0_ffn_wg': _L0_ffn_in['wg'], 'L0_ffn_wu': _L0_ffn_in['wu'], 'L0_ffn_wd': _L0_ffn_in['wd'], 'L0_ffn_swg': _L0_ffn_in['swg'], 'L0_ffn_swu': _L0_ffn_in['swu'], 'L0_ffn_swd': _L0_ffn_in['swd']}
    _x0 = _d['L0_attn_x']
    _d['L0_attn_x'] = jax.random.normal(jax.random.fold_in(jax.random.key(seed), 1), (2, 1024, 512), dtype=_x0.dtype)
    del _x0
    return _d

def reference(L0_attn_x, L0_attn_wq, L0_attn_wk, L0_attn_wv, L0_attn_wo, L0_ffn_router_w, L0_ffn_router_bias, L0_ffn_wg, L0_ffn_wu, L0_ffn_wd, L0_ffn_swg, L0_ffn_swu, L0_ffn_swd):

    def _L0_attn_ref(x, wq, wk, wv, wo):
        import math
        import jax, jax.numpy as jnp
        import numpy as np
        B, T, D = (2, 512, 512)
        NH, NKV = (32, 8)
        HD = D // NH
        bsz, seqlen, _ = x.shape
        q = (x @ wq).reshape(bsz, seqlen, NH, HD).transpose(0, 2, 1, 3)
        k = (x @ wk).reshape(bsz, seqlen, NKV, HD).transpose(0, 2, 1, 3)
        v = (x @ wv).reshape(bsz, seqlen, NKV, HD).transpose(0, 2, 1, 3)
        rep = NH // NKV
        k = jnp.repeat(k, rep, axis=1)
        v = jnp.repeat(v, rep, axis=1)
        att = jnp.einsum('bhqd,bhkd->bhqk', q.astype(jnp.float32), k.astype(jnp.float32)) / math.sqrt(HD)
        mask = jnp.triu(jnp.ones((seqlen, seqlen), dtype=bool), k=1)
        att = jnp.where(mask[None, None, :, :], -jnp.inf, att)
        att = jax.nn.softmax(att, axis=-1)
        y = jnp.einsum('bhqk,bhkd->bhqd', att, v.astype(jnp.float32)).astype(q.dtype)
        y = y.transpose(0, 2, 1, 3).reshape(bsz, seqlen, NH * HD)
        return y @ wo

    def _L0_ffn_ref(x, router_w, router_bias, wg, wu, wd, swg, swu, swd):
        import jax, jax.numpy as jnp
        import numpy as np
        B, T, D = (2, 256, 512)
        E, F, K = (64, 128, 4)
        S, HS = (2, 128 * 4)
        b, t, d = x.shape
        flat = x.reshape(b * t, d)
        n = flat.shape[0]
        logits = flat @ router_w
        scores = jax.nn.softmax(logits, axis=-1)
        _, topk_idx = jax.lax.top_k(logits + router_bias, K)
        topk_scores = jnp.take_along_axis(scores, topk_idx, axis=-1)
        topk_scores = topk_scores / topk_scores.sum(axis=-1, keepdims=True)
        comb = jnp.zeros((n, E), dtype=flat.dtype).at[jnp.arange(n)[:, None], topk_idx].set(topk_scores)
        g = jax.nn.silu(jnp.einsum('nd,edf->nef', flat, wg))
        u = jnp.einsum('nd,edf->nef', flat, wu)
        routed = jnp.einsum('ne,nef,efd->nd', comb, g * u, wd)
        sg = jax.nn.silu(jnp.einsum('nd,sdh->nsh', flat, swg))
        su = jnp.einsum('nd,sdh->nsh', flat, swu)
        shared = jnp.einsum('nsh,shd->nd', sg * su, swd)
        return (routed + shared).reshape(b, t, d)
    x = L0_attn_x
    x = x + _L0_attn_ref(_layernorm(x, axis=-1), L0_attn_wq, L0_attn_wk, L0_attn_wv, L0_attn_wo)
    x = x + _L0_ffn_ref(_layernorm(x, axis=-1), L0_ffn_router_w, L0_ffn_router_bias, L0_ffn_wg, L0_ffn_wu, L0_ffn_wd, L0_ffn_swg, L0_ffn_swu, L0_ffn_swd)
    return x

_drawn_inputs = setup_inputs


def setup_inputs(seed=0):
    import zlib

    import numpy as np

    out = dict(_drawn_inputs(seed))
    spreads = {'L0_ffn_router_bias': (0.0, 0.8)}
    factors = {'L0_ffn_router_w': 4.74, 'L0_ffn_wg': 4.656, 'L0_ffn_wu': 4.544, 'L0_ffn_wd': 4.568}
    for name, (base, spread) in spreads.items():
        noise = np.random.default_rng([zlib.crc32(name.encode()), seed]).standard_normal(out[name].shape)
        drawn = base * np.exp(spread * noise) if base else spread * noise
        out[name] = jnp.asarray(drawn.astype(out[name].dtype))
    for name, factor in factors.items():
        out[name] = (out[name] * factor).astype(out[name].dtype)
    return out
```

```python
import concourse.bass as bass
from concourse import mybir
from contextlib import ExitStack

FP32 = mybir.dt.float32
BF16 = mybir.dt.bfloat16
U32 = mybir.dt.uint32
ACT = mybir.ActivationFunctionType
ALU = mybir.AluOpType
AXX = mybir.AxisListType.X

P = 128
BATCH, SEQ, D = 2, 1024, 512
NTOK = BATCH * SEQ
NT = NTOK // P
C = D // P
HEADS, KVH, HD = 32, 8, 16
REP = HEADS // KVH
QT = SEQ // P
BANK = 512
E, F, TOPK = 64, 128, 4
HID = 1024
HC = HID // P
SLOT_TILES = -(-((TOPK * NTOK - E) // P + E) // 4) * 4
SLOTS = SLOT_TILES * P
EPS = 1e-5
NEG = -1e30

Q_PART = [0, 0, 1, 1, 0, 2]
K_PART = [0, 1, 0, 1, 2, 0]
STACK = len(Q_PART) * HD
KROWS = STACK + 2

HALF = SEQ // 2
WIN = SEQ // REP


def steps_of_half(half):
    full, odd = [], []
    for kt in range((half + 1) * HALF // P):
        q = max(kt * P, half * HALF)
        if q % WIN:
            odd.append((kt, q, P))
            q += P
        full += [[(kt, a, WIN, 0)] for a in range(q, (half + 1) * HALF, WIN)]
    pairs = [[(*odd[n], 0), (*odd[n + 1], REP * P)] for n in range(0, len(odd), 2)]
    return full + pairs


STEPS = steps_of_half(0) + steps_of_half(1)
NS = len(STEPS)
NS0 = len(steps_of_half(0))
PIECES = [(qt, lo, min(512, (qt + 1) * P - lo)) for qt in range(QT) for lo in range(0, (qt + 1) * P, 512)]
SIDE = REP * len(PIECES) + 1
MASKS = sum(x[0][1] == x[0][0] * P for x in STEPS)
PER_STEP = -(-(SIDE - 1) // (NS - 2))


def wait(eng, sem, value):
    if not (isinstance(value, int) and value <= 0):
        eng.wait_ge(sem, value)


def wait_alone(eng, sem, value, passed):
    eng.wait_ge(sem, value)
    eng.sem_inc(passed, 1)


def build_block(nc, x, wq, wk, wv, wo, router_w, router_bias, wg, wu, wd, swg, swu, swd, out):
    ctx = ExitStack()
    with ctx:
        def sb(name, shape, dt=FP32):
            return ctx.enter_context(nc.sbuf_tensor(name, shape, dt))

        def sem(name):
            return ctx.enter_context(nc.semaphore(name))

        def carve(arena, at, shape, dt=FP32):
            n = 1
            for d in shape[1:]:
                n *= d
            words = n * (2 if dt == BF16 else 4) // 4
            v = arena[0:shape[0], at:at + words]
            if dt != FP32:
                v = v.bitcast(dt)
            if len(shape) == 3:
                v = v.rearrange("p (a b) -> p a b", a=shape[1])
            if len(shape) == 4:
                v = v.rearrange("p (a b c) -> p a b c", a=shape[1], b=shape[2])
            return v, at + words

        def carve_all(arena, at, *wanted):
            views = []
            for shape, dt in wanted:
                v, at = carve(arena, at, shape, dt)
                views.append(v)
            return views

        qk_parts = nc.dram_tensor("qk_parts", [3, D + KVH * HD, NTOK], BF16)
        xn2_rows = nc.dram_tensor("xn2_rows", [NTOK, D], FP32)
        slot_tokens = nc.dram_tensor("slot_tokens", [SLOTS, 1], U32)
        slot_y = nc.dram_tensor("slot_y", [SLOTS, D], FP32)

        X = sb("X", [P, NT, D])
        XN = sb("XN", [P, NT, D])
        XT = sb("XT", [P, C, NTOK])
        att = sb("att", [P, 14336])
        w_att = sb("w_att", [P, 5120])
        ring = sb("ring", [P, 4 * 3 * C * F])
        small = sb("small", [P, 1536])
        ident = sb("ident", [P, P])
        eps_s = sb("eps_s", [P, 1])
        stats = sb("stats", [P, NT, 6])
        mv = sb("mv", [P, NT, 2])
        std = sb("std", [P, NT])
        rstd = sb("rstd", [P, NT])
        v_head = [sb(f"v_head{b}", [P, QT, 2 * HD]) for b in range(BATCH)]
        maxes = sb("maxes", [P, REP, QT])
        max_low = sb("max_low", [P, REP, QT // 2])
        max_rows = sb("max_rows", [REP * QT, 2, P], BF16)
        recip = sb("recip", [P, HALF // 32])
        router_s = sb("router_s", [P, C, E])
        bias_s = sb("bias_s", [P, E])

        wq_s, wk_s, wv_s, wo_s = carve_all(w_att, 0, ([P, C, D], FP32), ([P, C, KVH * HD], FP32),
                                           ([P, C, KVH * HD], FP32), ([P, C, D], FP32))
        v_all = carve(ring, 0, [P, NT, KVH * HD])[0].rearrange("p t (k d) -> p t k d", k=KVH)
        probs, *stacks = carve_all(att, 0, ([P, 4, REP * WIN], FP32), *[([P, REP, SEQ], BF16)] * 4,
                                   *[([P, SEQ], BF16)] * 4)
        q_max, q_exp, k_max, k_exp = stacks[0:2], stacks[2:4], stacks[4:6], stacks[6:8]
        stage, rest = carve_all(att, 0, ([P, 2, 3 * BANK], BF16), ([P, BANK], FP32))
        stage = stage.rearrange("p n (a t) -> p n a t", a=3)
        turned, causal, junk = carve_all(small, 0, ([P, HALF], FP32), ([P, BANK], FP32), ([P, 2, BANK], BF16))
        Z = XN[:, :, :].rearrange("p n d -> p (n d)").rearrange("p (b k h e) -> p b k h e", b=BATCH, h=KVH, e=HD)
        YT = XT

        flat_xn = XN[:, :, :].rearrange("p n d -> p (n d)")
        flat_xt = XT[:, :, :].rearrange("p c t -> p (c t)")
        XT2 = flat_xn.rearrange("p (c t) -> p c t", c=C)
        xn2, = carve_all(w_att, 0, ([P, 4, D], FP32))
        swg_s, swu_s, swd_s, tmp, mask, cum = carve_all(
            att, 0, ([P, 2 * C, D], FP32), ([P, 2 * C, D], FP32), ([P, HC, D], FP32), ([P, NT, E], FP32),
            ([P, NT, E], BF16), ([P, NT, E], BF16))
        hidden, biased, ex, *onehot = carve_all(
            flat_xt, 0, ([P, HC, BANK], FP32), ([P, NT, E], FP32), ([P, NT, E], FP32), *[([P, NT, E], BF16)] * TOPK)
        pos = biased
        silu_s, = carve_all(w_att, 4096, ([P, 2, BANK], FP32))
        (tri, ones_b, iota_e, top8, idx8, idxf, part_k, gates, slot_u, tab, tab_t, lmax, counts, start_s, row_e, iota_p,
         total_b, tiles_b, iota_c, token_ids) = carve_all(
            small, 0, ([P, P], BF16), ([P, P], BF16), ([P, E], FP32), ([P, NT, 8], FP32), ([P, NT, 8], U32),
            ([P, NT, 8], FP32), ([P, TOPK, NT], FP32), ([P, TOPK, NT], FP32), ([P, TOPK, NT], U32),
            ([P, P], U32), ([P, SLOT_TILES], U32), ([P, NT], FP32), ([P, 8], FP32), ([P, E], FP32), ([P, P], U32),
            ([P, 2], FP32), ([P, E], BF16), ([P, P], BF16), ([P, NT], FP32), ([P, NT], U32))
        ring_w = [carve(ring, j * 3 * C * F, [P, 3, C * F])[0] for j in range(4)]
        xg, xgt, yb, sg, hg = carve_all(w_att, 0, ([P, 4, D], FP32), ([P, 2, D], FP32), ([P, 2, D], FP32),
                                        ([P, 2, P], FP32), ([P, 2, P], FP32))
        idx = sb("idx", [P, 4], U32)
        yk = flat_xn.rearrange("p (t k d) -> p t k d", t=4, k=TOPK)

        PS = ctx.enter_context(nc.psum_tensor("PS", [P, 8 * BANK], FP32))

        def bank(k, n=BANK):
            return PS[:, k * BANK:k * BANK + n]

        x_in = [sem(f"x_in{g}") for g in range(4)]
        w_in = sem("w_in")
        pool_passed = sem("pool_passed")
        dve_passed = sem("dve_passed")
        eps_set = sem("eps_set")
        ident_zero = sem("ident_zero")
        ident_set = sem("ident_set")
        causal_zero = sem("causal_zero")
        causal_set = sem("causal_set")
        v_ones = sem("v_ones")
        k_ones = sem("k_ones")
        ln_stats = sem("ln_stats")
        ln_aggr = sem("ln_aggr")
        ln_std = sem("ln_std")
        ln_rstd = sem("ln_rstd")
        xn_ready = sem("xn_ready")
        prep_done = sem("prep_done")
        prep_read = [sem(f"prep_read{k}") for k in range(8)]
        xt_ready = [sem("xt_ready_dve"), sem("xt_ready_act")]
        part_hi = sem("part_hi")
        part_rest = sem("part_rest")
        part_mid = sem("part_mid")
        part_low = sem("part_low")
        parts_out = [sem("parts_out0"), sem("parts_out1")]
        v_done = sem("v_done")

        max_in = [sem("max_in0"), sem("max_in1")]
        exp_in = [sem("exp_in0"), sem("exp_in1")]
        v_in = [sem("v_in0"), sem("v_in1")]
        side_done = sem("side_done")
        side_read = sem("side_read")
        reduced = sem("reduced")
        max_ready = sem("max_ready")
        max_hi = sem("max_hi")
        rows_ready = sem("rows_ready")
        rows_in = sem("rows_in")
        scores_done = sem("scores_done")
        exp_done = sem("exp_done")
        masked = sem("masked")
        pv_done = sem("pv_done")
        turn_done = sem("turn_done")
        recip_done = sem("recip_done")
        z_done = sem("z_done")
        yt_done = sem("yt_done")

        shared_in = sem("shared_in")
        x1_done = sem("x1_done")
        ln2_stats = sem("ln2_stats")
        ln2_aggr = sem("ln2_aggr")
        ln2_std = sem("ln2_std")
        ln2_rstd = sem("ln2_rstd")
        wo_done = sem("wo_done")
        xn2_ready = sem("xn2_ready")
        xn2_stored = sem("xn2_stored")
        turn2_done = sem("turn2_done")
        xt2_ready = sem("xt2_ready")
        logits_done = sem("logits_done")
        consts = sem("consts")
        route = sem("route")
        ex_ready = sem("ex_ready")
        masks_ready = sem("masks_ready")
        ranks_done = sem("ranks_done")
        tiles_ready = sem("tiles_ready")
        starts_done = sem("starts_done")
        slots_ready = sem("slots_ready")
        table_zero = sem("table_zero")
        table_set = sem("table_set")
        table_in = sem("table_in")
        table_float = sem("table_float")
        table_turned = sem("table_turned")
        table_ready = sem("table_ready")
        experts_ready = sem("experts_ready")
        experts_in = sem("experts_in")
        up_done = sem("up_done")
        silu_done = sem("silu_done")
        hidden_done = sem("hidden_done")
        down_done = sem("down_done")
        shared_added = sem("shared_added")

        ring_in = [sem(f"ring_in{j}") for j in range(4)]
        idx_set = sem("idx_set")
        xg_in = [sem(f"xg_in{j}") for j in range(4)]
        xg_turned = sem("xg_turned")
        xgt_ready = sem("xgt_ready")
        e_up = sem("e_up")
        e_silu = sem("e_silu")
        e_hidden = sem("e_hidden")
        e_down = sem("e_down")
        yb_ready = sem("yb_ready")
        yb_stored = [sem("yb_stored0"), sem("yb_stored1")]
        yk_in = [sem(f"yk_in{n}") for n in range(4)]
        mixed = sem("mixed")
        stored = sem("stored")

        x_view = x.rearrange("b (n p) d -> p (b n) d", p=P)
        out_view = out.rearrange("b (n p) d -> p (b n) d", p=P)

        jobs = [("T", t) for t in range(4)]
        for g in range(4):
            jobs += [("T", t) for t in range(4 * g + 4, min(4 * g + 8, NT))]
            jobs += [("QK", (m, g)) for m in range(C + 1)] + [("V", g)]
        QK_JOBS = (C + 1) * 4

        block = ctx.enter_context(nc.Block())

        @block.sync
        def _(sp):
            for g in range(4):
                sp.dma_start(X[:, 4 * g:4 * g + 4, :], x_view[:, 4 * g:4 * g + 4, :]).then_inc(x_in[g], 16)
            for n, (m, g) in enumerate([a for k, a in jobs if k == "QK"]):
                sp.wait_ge(part_low, n + 1)
                sp.dma_start(qk_parts[:, m * P:(m + 1) * P, g * BANK:(g + 1) * BANK].rearrange("a p t -> p a t"),
                             stage[:, n % 2, :, :]).then_inc(parts_out[n % 2], 16)
            for s in parts_out:
                sp.wait_ge(s, 16 * QK_JOBS // 2)

            def load_stack(q, k, i, b, done):
                at = slice(b * SEQ, (b + 1) * SEQ)
                for j in range(len(Q_PART)):
                    sp.dma_start(q[b][j * HD:(j + 1) * HD, :, :],
                                 qk_parts[Q_PART[j], bass.ds(i * (REP * HD), REP * HD), at]
                                 .rearrange("(r d) t -> d r t", r=REP)).then_inc(done[b], 16)
                    sp.dma_start(k[b][j * HD:(j + 1) * HD, :],
                                 qk_parts[K_PART[j], bass.ds(i * HD + D, HD), at]).then_inc(done[b], 16)

            def group(i, b, last):
                g = BATCH * i + b
                if not last:
                    sp.wait_ge(side_done, SIDE * g + SIDE - 1)
                    load_stack(q_max, k_max, i + 1, b, max_in)
                if not (last and b == BATCH - 1):
                    sp.wait_ge(rows_ready, g + 2)
                    for h in range(2):
                        sp.dma_start(q_exp[1 - b][STACK + h:STACK + h + 1, :, :], max_rows[:, h, :])\
                          .then_inc(rows_in, 16)
                if not last:
                    sp.wait_ge(scores_done, NS * (g + 1))
                    load_stack(q_exp, k_exp, i + 1, b, exp_in)

            for b in range(BATCH):
                load_stack(q_max, k_max, 0, b, max_in)
                load_stack(q_exp, k_exp, 0, b, exp_in)
            sp.wait_ge(rows_ready, 1)
            for h in range(2):
                sp.dma_start(q_exp[0][STACK + h:STACK + h + 1, :, :], max_rows[:, h, :]).then_inc(rows_in, 16)
            for b in range(BATCH):
                group(0, b, False)
            with sp.Fori(1, KVH - 1) as i:
                for b in range(BATCH):
                    group(i, b, False)
            for b in range(BATCH):
                group(KVH - 1, b, True)
            sp.wait_ge(z_done, 4 * KVH)
            for dst, src in ((swg_s, swg), (swu_s, swu)):
                sp.dma_start(dst.rearrange("p (s c) n -> p s c n", s=2), src.rearrange("s (c p) n -> p s c n", p=P))\
                  .then_inc(shared_in, 16)
            sp.dma_start(swd_s.rearrange("p (s c) n -> p s c n", s=2), swd.rearrange("s (c p) n -> p s c n", p=P))\
              .then_inc(shared_in, 16)
            for t in range(NT):
                sp.wait_ge(xn2_ready, t + 1)
                sp.dma_start(xn2_rows[t * P:(t + 1) * P, :], xn2[:, t % 4, :]).then_inc(xn2_stored, 16)
            sp.wait_ge(experts_ready, 1)
            sp.dma_start(row_e[0:1, :], counts[:, 4:5].bitcast(U32)).then_inc(experts_in, 16)
            sp.wait_ge(table_set, 16 * TOPK * NT)
            sp.dma_start(tab[:, :], slot_tokens.rearrange("(s p) o -> s (p o)", p=P)).then_inc(table_in, 16)

            def load_expert(i, j):
                n = 4 * i + j
                e = sp.value_load(row_e[0:1, bass.ds(n, 1)], min_val=0, max_val=E - 1)
                wait(sp, e_down, n - 3)
                for k, w in enumerate((wg, wu)):
                    sp.dma_start(ring_w[j][:, k, :], w[bass.ds(e, 1), :, :].rearrange("o (p c) f -> p (o c f)", c=C))\
                      .then_inc(ring_in[j], 16)
                sp.dma_start(ring_w[j][:, 2, :], wd[bass.ds(e, 1), :, :].rearrange("o f d -> f (o d)"))\
                  .then_inc(ring_in[j], 16)

            sp.wait_ge(experts_in, 16)
            for j in range(4):
                load_expert(0, j)
            with sp.Fori(1, SLOT_TILES // 4) as i:
                for j in range(4):
                    load_expert(i, j)
            for t in range(NT):
                sp.wait_ge(mixed, TOPK * (t + 1))
                sp.dma_start(out_view[:, t, :], X[:, t, :]).then_inc(stored, 16)
            sp.wait_ge(stored, 16 * NT)

        @block.gpsimd
        def _(pool):
            pool.memset(eps_s[:, :], EPS).then_inc(eps_set, 1)
            pool.memset(ident[:, :], 0.0).then_inc(ident_zero, 1)
            pool.wait_ge(ident_zero, 1)
            pool.affine_select(out=ident[:, :], in_=ident[:, :], compare_op=ALU.not_equal, fill=1.0, base=0,
                               pattern=[[-1, P]], channel_multiplier=1).then_inc(ident_set, 1)
            for b in range(BATCH):
                pool.memset(v_head[b][:, :, :], 1.0).then_inc(v_ones, 1)
            pool.memset(causal[:, :], 0.0).then_inc(causal_zero, 1)
            pool.wait_ge(causal_zero, 1)
            pool.affine_select(out=causal[:, BANK - P:], in_=causal[:, BANK - P:], compare_op=ALU.is_ge, fill=NEG,
                               base=0, pattern=[[-1, P]], channel_multiplier=1).then_inc(causal_set, 1)
            pool.wait_ge(causal_set, 1)
            for b in range(BATCH):
                pool.memset(k_exp[b][STACK:KROWS, :], 1.0).then_inc(k_ones, 1)
                pool.wait_ge(k_ones, b + 1)

            def load_v(i, b):
                pool.tensor_copy(v_head[b][:, :, 0:HD], v_all[:, b * QT:(b + 1) * QT, bass.ds(i, 1), :]
                                 .rearrange("p t o e -> p t (o e)")).then_inc(v_in[b], 1)

            def group(i, b, last):
                g = BATCH * i + b
                for s, segments in enumerate(STEPS):
                    if s == 3 and not (last and b == 1):
                        wait(pool, pv_done, NS * g)
                        load_v(i + b, 1 - b)
                    if segments[0][1] - segments[0][0] * P not in (0,):
                        continue
                    wait_alone(pool, exp_done, NS * g + s + 1, pool_passed)
                    n = len(segments) * REP
                    d = probs[:, (NS * b + s) % 4, :].rearrange("p (r q) -> p r q", r=n)[:, :, 0:P]
                    pool.affine_select(out=d, in_=d, compare_op=ALU.is_ge, fill=0.0, base=0,
                                       pattern=[[0, n], [1, P]], channel_multiplier=-1).then_inc(masked, 1)

            pool.wait_ge(v_done, 4)
            pool.wait_ge(v_ones, 2)
            load_v(0, 0)
            for b in range(BATCH):
                group(0, b, False)
            with pool.Fori(1, KVH - 1) as i:
                for b in range(BATCH):
                    group(i, b, False)
            for b in range(BATCH):
                group(KVH - 1, b, True)

            pool.wait_ge(z_done, 4 * KVH)
            pool.wait_ge(side_read, SIDE * BATCH * KVH)
            pool.memset(ones_b[:, :], 1.0).then_inc(consts, 1)
            pool.memset(tri[:, :], 1.0).then_inc(consts, 1)
            pool.wait_ge(consts, 2)
            pool.affine_select(out=tri[:, :], in_=tri[:, :], compare_op=ALU.is_gt, fill=0.0, base=0,
                               pattern=[[1, P]], channel_multiplier=-1).then_inc(consts, 1)
            pool.iota(top8[:, 0:8, :].rearrange("p a b -> p (a b)").bitcast(U32), pattern=[[1, E]], base=0,
                      channel_multiplier=0).then_inc(consts, 1)
            pool.iota(top8[:, 8:9, 0:1].rearrange("p a b -> p (a b)").bitcast(U32), pattern=[[1, 1]], base=0,
                      channel_multiplier=1).then_inc(consts, 1)
            pool.iota(idxf[:, 0:2, :].rearrange("p a b -> p (a b)").bitcast(U32), pattern=[[P, NT]], base=0,
                      channel_multiplier=0).then_inc(consts, 1)
            pool.iota(token_ids[:, :], pattern=[[P, NT]], base=0, channel_multiplier=1).then_inc(consts, 1)
            pool.memset(tab[:, :], 0).then_inc(consts, 1)
            pool.wait_ge(consts, 8)
            pool.tensor_copy(iota_e[:, :], top8[:, 0:8, :].rearrange("p a b -> p (a b)").bitcast(U32)).then_inc(consts, 1)
            pool.tensor_copy(iota_p[:, 0:1], top8[:, 8:9, 0:1].rearrange("p a b -> p (a b)").bitcast(U32)).then_inc(consts, 1)
            pool.tensor_copy(iota_c[:, :], idxf[:, 0:2, :].rearrange("p a b -> p (a b)").bitcast(U32)).then_inc(consts, 1)
            pool.wait_ge(consts, 11)
            pool.dma_start(slot_tokens.rearrange("(s p) o -> s (p o)", p=P), tab[:, :]).then_inc(table_zero, 16)
            pool.wait_ge(table_zero, 16)
            pool.wait_ge(slots_ready, 1)
            for k in range(TOPK):
                for t in range(NT):
                    pool.indirect_dma_start(out=slot_tokens[:, :],
                                            out_offset=bass.IndirectOffsetOnAxis(ap=slot_u[:, k, t:t + 1], axis=0),
                                            in_=token_ids[:, t:t + 1], in_offset=None).then_inc(table_set, 16)

            def gather_tokens(i, j):
                n = 4 * i + j
                wait(pool, xg_turned, n - 3)
                pool.tensor_copy(idx[:, j:j + 1], tab_t[:, bass.ds(n, 1)]).then_inc(idx_set, 1)
                wait_alone(pool, idx_set, n + 1, pool_passed)
                pool.indirect_dma_start(out=xg[:, j, :], out_offset=None, in_=xn2_rows[:, :],
                                        in_offset=bass.IndirectOffsetOnAxis(ap=idx[:, j:j + 1], axis=0))\
                    .then_inc(xg_in[j], 16)

            pool.wait_ge(table_ready, 1)
            pool.wait_ge(xn2_stored, 16 * NT)
            for j in range(4):
                gather_tokens(0, j)
            with pool.Fori(1, SLOT_TILES // 4) as i:
                for j in range(4):
                    gather_tokens(i, j)
            for s in yb_stored:
                pool.wait_ge(s, 16 * SLOT_TILES // 2)
            for t in range(NT):
                if t >= 4:
                    pool.wait_ge(mixed, TOPK * (t - 3))
                for k in range(TOPK):
                    pool.indirect_dma_start(out=yk[:, t % 4, k, :], out_offset=None, in_=slot_y[:, :],
                                            in_offset=bass.IndirectOffsetOnAxis(ap=slot_u[:, k, t:t + 1], axis=0))\
                        .then_inc(yk_in[t % 4], 16)

        @block.scalar
        def _(act):
            for dst, src in ((wk_s, wk), (wv_s, wv), (wq_s, wq), (wo_s, wo)):
                if dst is not wo_s:
                    act.dma_start(dst[:, :, :], src.rearrange("(c p) n -> p c n", p=P)).then_inc(w_in, 16)
            wo_rows = wo.rearrange("(c k r d) n -> r k d c n", k=2, r=REP, d=HD)
            for r in range(REP):
                for k in range(2):
                    at = (2 * r + k) * HD
                    act.dma_start(wo_s[at:at + HD, :, :], wo_rows[r, k]).then_inc(w_in, 16)
            act.dma_start(router_s[:, :, :], router_w.rearrange("(c p) e -> p c e", p=P)).then_inc(w_in, 16)
            act.dma_start(bias_s[:, :], router_bias.partition_broadcast(P)).then_inc(w_in, 16)
            act.wait_ge(eps_set, 1)

            def deviation(g):
                act.wait_ge(ln_aggr, g + 1)
                act.activation(std[:, 4 * g:4 * g + 4], mv[:, 4 * g:4 * g + 4, 1], ACT.Sqrt, bias=eps_s[:, :])\
                   .then_inc(ln_std, 1)

            deviation(0)
            qk = 0
            for j, (kind, a) in enumerate(jobs):
                if kind == "T" and a % 4 == 0 and a + 4 < NT:
                    deviation(a // 4 + 1)
                if kind == "T" and a % 2 == 1:
                    act.wait_ge(prep_done, j + 1)
                    act.activation(XT[:, :, a * P:(a + 1) * P], bank(j % 8).rearrange("p (c t) -> p c t", c=C),
                                   ACT.Copy).then_inc(xt_ready[1], 1)
                    pass
                if kind == "QK":
                    act.wait_ge(prep_done, j + 1)
                    if qk >= 2:
                        act.wait_ge(parts_out[qk % 2], 16 * (qk // 2))
                    act.activation(stage[:, qk % 2, 0, :], bank(j % 8), ACT.Copy).then_inc(part_hi, 1)
                    qk += 1

            def exps(i):
                for n0 in range(BATCH * NS):
                    n = BATCH * NS * i + n0
                    act.wait_ge(scores_done, n + 1)
                    wait(act, pv_done, n - 3)
                    act.activation(probs[:, n0 % 4, :], PS[:, (n0 % 2) * 2 * BANK:(n0 % 2 + 1) * 2 * BANK], ACT.Exp,
                                   scale=HD ** -0.5).then_inc(exp_done, 1)

            exps(0)
            with act.Fori(1, KVH - 1) as i:
                exps(i)
            exps(KVH - 1)

            for g in range(4):
                act.wait_ge(ln2_aggr, g + 1)
                act.activation(std[:, 4 * g:4 * g + 4], mv[:, 4 * g:4 * g + 4, 1], ACT.Sqrt, bias=eps_s[:, :])\
                   .then_inc(ln2_std, 1)
                for t in range(4 * g, 4 * g + 4):
                    act.wait_ge(turn2_done, t + 1)
                    act.activation(XT2[:, :, t * P:(t + 1) * P], bank(4 + t % 2).rearrange("p (c t) -> p c t", c=C),
                                   ACT.Copy).then_inc(xt2_ready, 1)
            act.wait_ge(route, 2)
            act.activation(ex[:, :, :], tmp[:, :, :], ACT.Exp).then_inc(ex_ready, 1)
            for n in range(4 * HC):
                act.wait_ge(up_done, n + 1)
                if n >= 2:
                    act.wait_ge(hidden_done, n - 1)
                act.activation(silu_s[:, n % 2, :], bank(2 * (n % 2)), ACT.Silu).then_inc(silu_done, 1)

            def turned_tokens(n, k):
                act.wait_ge(xg_turned, n + 1)
                wait(act, e_up, n - 1)
                act.activation(xgt[:, k % 2, :], bank(k % 2), ACT.Copy).then_inc(xgt_ready, 1)

            def silu(n, k):
                act.wait_ge(e_up, n + 1)
                wait(act, e_hidden, n - 1)
                act.activation(sg[:, k % 2, :], bank(2 + k % 2, F), ACT.Silu).then_inc(e_silu, 1)

            def store_y(n, k):
                act.wait_ge(yb_ready, n + 1)
                act.dma_start(slot_y[bass.ds(n * P, P), :], yb[:, k % 2, :]).then_inc(yb_stored[k % 2], 16)

            def expert_tiles(i, first, last):
                for j in range(4):
                    n = 4 * i + j
                    if not (last and j == 3):
                        turned_tokens(n + 1, j + 1)
                    silu(n, j)
                    if not (first and j < 2):
                        store_y(n - 2, j - 2)

            turned_tokens(0, 0)
            expert_tiles(0, True, False)
            with act.Fori(1, SLOT_TILES // 4 - 1) as i:
                expert_tiles(i, False, False)
            expert_tiles(SLOT_TILES // 4 - 1, False, True)
            store_y(SLOT_TILES - 2, 0)
            store_y(SLOT_TILES - 1, 1)
            for s in yb_stored:
                act.wait_ge(s, 16 * SLOT_TILES // 2)

        @block.tensor
        def _(pe):
            pe.wait_ge(ident_set, 1)
            seen = {}
            for j, (kind, a) in enumerate(jobs):
                if j >= 8:
                    pk, pa = jobs[j - 8]
                    if pk == "T":
                        pe.wait_ge(xt_ready[pa % 2], pa // 2 + 1)
                    elif pk == "QK":
                        pe.wait_ge(part_rest, seen[j - 8] + 1)
                    else:
                        pe.wait_ge(v_done, pa + 1)
                if kind == "T":
                    pe.wait_ge(xn_ready, a + 1)
                    for c in range(C):
                        mm = pe.transpose(PS[:, (j % 8) * BANK + c * P:(j % 8) * BANK + (c + 1) * P],
                                          XN[:, a, c * P:(c + 1) * P], ident[:, :])
                elif kind == "QK":
                    m, g = a
                    seen[j] = (C + 1) * g + m
                    if m == 0:
                        pe.wait_ge(w_in, 16 * 13)
                        for s in xt_ready:
                            pe.wait_ge(s, 2 * g + 2)
                    for c in range(C):
                        w = wq_s[:, c, m * P:(m + 1) * P] if m < C else wk_s[:, c, :]
                        mm = pe.matmul(bank(j % 8), w, XT[:, c, g * BANK:(g + 1) * BANK],
                                       start=(c == 0), stop=(c == C - 1))
                else:
                    for t in range(4):
                        for c in range(C):
                            mm = pe.matmul(PS[:, (j % 8) * BANK + t * P:(j % 8) * BANK + (t + 1) * P],
                                           XT[:, c, (4 * a + t) * P:(4 * a + t + 1) * P], wv_s[:, c, :],
                                           start=(c == 0), stop=(c == C - 1))
                mm.then_inc(prep_done, 1)

            def piece(b, k, index, parity):
                wait(pe, side_read, index - 1)
                qt, lo, n = PIECES[k % len(PIECES)]
                pe.matmul(bank(4 + parity % 2, n), q_max[b][0:STACK, k // len(PIECES), qt * P:(qt + 1) * P],
                          k_max[b][0:STACK, lo:lo + n], start=True, stop=True).then_inc(side_done, 1)

            def turn(g, index, parity):
                pe.wait_ge(max_ready, g + 1)
                wait(pe, side_read, index - 1)
                pe.transpose(bank(4 + parity % 2, P)[0:REP * QT, :], maxes[:, :, :].rearrange("p r t -> p (r t)"),
                             ident[:, :]).then_inc(side_done, 1)

            def side(i, b, s, part):
                g = BATCH * i + b
                if s == 0 and part == 0:
                    pe.wait_ge(max_in[b], 16 * 2 * len(Q_PART) * (i + 1))
                for k in range(s * PER_STEP + part, min(s * PER_STEP + part + 1, SIDE)):
                    index, parity = SIDE * g + k, SIDE * b + k
                    if k < SIDE - 1:
                        piece(b, k, index, parity)
                    else:
                        turn(g, index, parity)

            def scores(i, b, s, between=()):
                n, parity = NS * (BATCH * i + b) + s, (NS * b + s) % 2
                if s == 0:
                    pe.wait_ge(exp_in[b], 16 * 2 * len(Q_PART) * (i + 1))
                    pe.wait_ge(rows_in, 32 * (BATCH * i + b + 1))
                wait(pe, exp_done, n - 1)
                between = list(between)
                for kt, q0, qn, col in STEPS[s]:
                    rows = BANK // qn
                    for r in range(0, REP, rows):
                        if between and (kt, r) != (STEPS[s][0][0], 0):
                            side(*between)
                        at = parity * 2 * BANK + col + r * qn
                        mm = pe.matmul(PS[:, at:at + BANK], k_exp[b][0:KROWS, kt * P:(kt + 1) * P],
                                       q_exp[b][0:KROWS, r:r + rows, q0:q0 + qn], start=True, stop=True)
                mm.then_inc(scores_done, 1)

            def values(i, b, s):
                g = BATCH * i + b
                n = NS * g + s
                pe.wait_ge(exp_done, n + 1)
                if s == 0:
                    pe.wait_ge(v_in[b], i + 1)
                    wait(pe, turn_done, 2 * g - 1)
                if s == NS0:
                    wait(pe, turn_done, 2 * g)
                if STEPS[s][0][1] == STEPS[s][0][0] * P:
                    pe.wait_ge(masked, MASKS * g + sum(x[0][1] == x[0][0] * P for x in STEPS[:s + 1]))
                for kt, q0, qn, col in STEPS[s]:
                    for r in range(REP):
                        at = 6 * BANK + q0
                        a = col + r * qn
                        mm = pe.matmul(PS[32 * r:32 * r + 32, at:at + qn], v_head[b][:, kt, :],
                                       probs[:, (NS * b + s) % 4, a:a + qn], start=s in (0, NS0), stop=False,
                                       skip_group_check=True)
                mm.then_inc(pv_done, 1)

            def group(i, b, last):
                for s in range(NS):
                    more = not (last and b == 1)
                    if more:
                        side(i + b, 1 - b, s, 0)
                    between = (i + b, 1 - b, s, 1) if more else ()
                    if s + 1 < NS:
                        scores(i, b, s + 1, between)
                    elif more:
                        scores(i + b, 1 - b, 0, between)
                    if more:
                        side(i + b, 1 - b, s, 2)
                    values(i, b, s)

            pe.wait_ge(k_ones, 2)
            pe.wait_ge(v_done, 4)
            pe.wait_ge(part_rest, QK_JOBS)
            for s in range(NS):
                for part in range(PER_STEP):
                    side(0, 0, s, part)
            scores(0, 0, 0)
            for b in range(BATCH):
                group(0, b, False)
            with pe.Fori(1, KVH - 1) as i:
                for b in range(BATCH):
                    group(i, b, False)
            for b in range(BATCH):
                group(KVH - 1, b, True)

            def project(t):
                pe.wait_ge(yt_done, C * (t // QT + 1))
                if t == 0:
                    pe.wait_ge(exp_done, NS * BATCH * KVH)
                if t >= 4:
                    pe.wait_ge(x1_done, t - 3)
                for c in range(C):
                    mm = pe.matmul(bank(t % 4), YT[:, c, t * P:(t + 1) * P], wo_s[:, c, :],
                                   start=(c == 0), stop=(c == C - 1))
                mm.then_inc(wo_done, 1)

            def turn_tokens(t):
                pe.wait_ge(xn2_ready, t + 1)
                if t >= 2:
                    pe.wait_ge(xt2_ready, t - 1)
                for c in range(C):
                    mm = pe.transpose(PS[:, (4 + t % 2) * BANK + c * P:(4 + t % 2) * BANK + (c + 1) * P],
                                      xn2[:, t % 4, c * P:(c + 1) * P], ident[:, :])
                mm.then_inc(turn2_done, 1)

            def logits(t):
                pe.wait_ge(xt2_ready, t + 1)
                at = 6 * BANK + t * E
                for c in range(C):
                    mm = pe.matmul(PS[:, at:at + E], XT2[:, c, t * P:(t + 1) * P], router_s[:, c, :],
                                   start=(c == 0), stop=(c == C - 1))
                mm.then_inc(logits_done, 1)

            for g in range(5):
                if g < 4:
                    for t in range(4 * g, 4 * g + 4):
                        project(t)
                if g >= 1:
                    for t in range(4 * g - 4, 4 * g):
                        turn_tokens(t)
                    for t in range(4 * g - 4, 4 * g):
                        logits(t)

            pe.wait_ge(masks_ready, 1)
            for h in range(2):
                half = slice(h * NT // 2, (h + 1) * NT // 2)
                flat = lambda v: v[:, half, :].rearrange("p t e -> p (t e)")
                pe.matmul(bank(h), tri[:, :], flat(mask), start=True, stop=False)
                pe.matmul(bank(h), ones_b[:, :], flat(cum), start=False, stop=True)
            pe.matmul(bank(2, 1)[0:E, :], total_b[:, :], ones_b[:, 0:1], start=True, stop=True).then_inc(ranks_done, 1)
            pe.wait_ge(tiles_ready, 1)
            pe.matmul(bank(3, E), tiles_b[0:E, :], tri[0:E, 0:E], start=True, stop=True).then_inc(starts_done, 1)
            pe.wait_ge(slots_ready, 1)

            pe.wait_ge(shared_in, 48)
            for g in range(4):
                for hc in range(HC):
                    n = HC * g + hc
                    if n >= 2:
                        pe.wait_ge(hidden_done, n - 1)
                    s, at = hc // C, (hc % C) * P
                    for k, w in enumerate((swg_s, swu_s)):
                        for c in range(C):
                            mm = pe.matmul(bank(2 * (n % 2) + k), w[:, C * s + c, at:at + P],
                                           XT2[:, c, g * BANK:(g + 1) * BANK], start=(c == 0), stop=(c == C - 1))
                    mm.then_inc(up_done, 1)
                pe.wait_ge(hidden_done, HC * (g + 1))
                for t in range(4 * g, 4 * g + 4):
                    if t >= 2:
                        pe.wait_ge(shared_added, t - 1)
                    for hc in range(HC):
                        mm = pe.matmul(bank(4 + t % 2), hidden[:, hc, (t % 4) * P:(t % 4 + 1) * P], swd_s[:, hc, :],
                                       start=(hc == 0), stop=(hc == HC - 1))
                    mm.then_inc(down_done, 1)

            pe.wait_ge(table_float, 1)
            pe.transpose(bank(6, SLOT_TILES), tmp[:, 0:2, :].rearrange("p a b -> p (a b)"), ident[:, :])\
              .then_inc(table_turned, 1)

            def turn_slots(n, k):
                j = k % 4
                i = (n - j) // 4 if isinstance(n, int) else None
                pe.wait_ge(xg_in[j], 16 * (turn_count(n, k)))
                wait(pe, xgt_ready, n - 1)
                for c in range(C):
                    mm = pe.transpose(PS[:, (k % 2) * BANK + c * P:(k % 2) * BANK + (c + 1) * P],
                                      xg[:, j, c:D:C], ident[:, :])
                mm.then_inc(xg_turned, 1)

            def turn_count(n, k):
                return UNIT[0] + 1 + k // 4

            UNIT = [0]

            def expert_up(n, k):
                pe.wait_ge(ring_in[k % 4], 48 * (UNIT[0] + 1))
                pe.wait_ge(xgt_ready, n + 1)
                wait(pe, e_hidden, n - 1)
                for m in range(2):
                    for c in range(C):
                        at = (2 + k % 2) * BANK + m * F
                        mm = pe.matmul(PS[:, at:at + P], ring_w[k % 4][:, m, c * F:(c + 1) * F],
                                       xgt[:, k % 2, c * P:(c + 1) * P], start=(c == 0), stop=(c == C - 1))
                mm.then_inc(e_up, 1)

            def expert_down(n, k):
                pe.wait_ge(e_hidden, n + 1)
                wait(pe, yb_ready, n - 1)
                pe.matmul(bank(4 + k % 2), hg[:, k % 2, :], ring_w[k % 4][:, 2, :], start=True, stop=True)\
                  .then_inc(e_down, 1)

            def expert_tiles(i, first, last):
                UNIT[0] = i
                for j in range(4):
                    n = 4 * i + j
                    if not (last and j == 3):
                        turn_slots(n + 1, j + 1)
                    expert_up(n, j)
                    if not (first and j == 0):
                        expert_down(n - 1, j - 1)

            turn_slots(0, 0)
            expert_tiles(0, True, False)
            with pe.Fori(1, SLOT_TILES // 4 - 1) as i:
                expert_tiles(i, False, False)
            expert_tiles(SLOT_TILES // 4 - 1, False, True)
            expert_down(SLOT_TILES - 1, 3)

        @block.vector
        def _(dve):
            def normalise_group(g):
                dve.wait_ge(x_in[g], 16)
                for t in range(4 * g, 4 * g + 4):
                    last = dve.bn_stats(stats[:, t, :], X[:, t, :])
                last.then_inc(ln_stats, 1)
                dve.wait_ge(ln_stats, g + 1)
                for t in range(4 * g, 4 * g + 4):
                    last = dve.bn_aggr(mv[:, t, :], stats[:, t, :])
                last.then_inc(ln_aggr, 1)
                dve.wait_ge(ln_std, g + 1)
                dve.reciprocal(rstd[:, 4 * g:4 * g + 4], std[:, 4 * g:4 * g + 4]).then_inc(ln_rstd, 1)
                dve.wait_ge(ln_rstd, g + 1)
                for t in range(4 * g, 4 * g + 4):
                    dve.tensor_scalar(XN[:, t, :], X[:, t, :], mv[:, t, 0:1], rstd[:, t:t + 1],
                                      ALU.subtract, ALU.mult).then_inc(xn_ready, 1)

            normalise_group(0)
            qk = 0
            for j, (kind, a) in enumerate(jobs):
                if kind == "T" and a % 4 == 0 and a // 4 + 1 < 4:
                    normalise_group(a // 4 + 1)
                if kind == "T" and a % 2 == 0:
                    dve.wait_ge(prep_done, j + 1)
                    dve.tensor_copy(XT[:, :, a * P:(a + 1) * P], bank(j % 8).rearrange("p (c t) -> p c t", c=C))\
                       .then_inc(xt_ready[0], 1)
                if kind == "QK":
                    dve.wait_ge(part_hi, qk + 1)
                    dve.tensor_tensor(rest[:, :], bank(j % 8), stage[:, qk % 2, 0, :], ALU.subtract)\
                       .then_inc(part_rest, 1)
                    dve.wait_ge(part_rest, qk + 1)
                    dve.tensor_copy(stage[:, qk % 2, 1, :], rest[:, :]).then_inc(part_mid, 1)
                    dve.wait_ge(part_mid, qk + 1)
                    dve.tensor_tensor(stage[:, qk % 2, 2, :], rest[:, :], stage[:, qk % 2, 1, :], ALU.subtract)\
                       .then_inc(part_low, 1)
                    dve.wait_ge(part_low, qk + 1)
                    qk += 1
                if kind == "V":
                    dve.wait_ge(prep_done, j + 1)
                    dve.tensor_copy(v_all[:, 4 * a:4 * a + 4, :, :],
                                    bank(j % 8).rearrange("p (t k d) -> p t k d", t=4, k=KVH)).then_inc(v_done, 1)

            def reduce_piece(k, index, parity):
                r = k // len(PIECES)
                qt, lo, n = PIECES[k % len(PIECES)]
                src = bank(4 + parity % 2, n)
                if lo + n == (qt + 1) * P:
                    wait_alone(dve, side_done, index + 1, dve_passed)
                    dve.tensor_tensor_reduce(out=junk[:, parity % 2, 0:n], in0=src, in1=causal[:, BANK - n:], scale=1.0,
                                             scalar=-3e38, op0=ALU.add, op1=ALU.max,
                                             accum_out=maxes[:, r, qt:qt + 1]).then_inc(side_read, 1)
                else:
                    dve.wait_ge(side_done, index + 1)
                    dve.reduce_max(max_low[:, r, qt - QT // 2:qt - QT // 2 + 1], src, AXX).then_inc(side_read, 1)

            def turn_rows(g, index, parity):
                dve.wait_ge(side_done, index + 1)
                src = bank(4 + parity % 2, P)[0:REP * QT, :]
                dve.tensor_scalar(max_rows[:, 0, :], src, -1.0, None, ALU.mult).then_inc(max_hi, 1)
                dve.wait_ge(max_hi, g + 1)
                dve.scalar_tensor_tensor(out=max_rows[:, 1, :], in0=src, scalar=-1.0, in1=max_rows[:, 0, :],
                                         op0=ALU.mult, op1=ALU.subtract).then_inc(side_read, 1)
                dve.wait_ge(side_read, index + 1)
                dve.sem_inc(rows_ready, 1)

            def side(i, b, s):
                g = BATCH * i + b
                for k in range(s * PER_STEP, min((s + 1) * PER_STEP, SIDE)):
                    index, parity = SIDE * g + k, SIDE * b + k
                    if k < SIDE - 1:
                        reduce_piece(k, index, parity)
                    else:
                        turn_rows(g, index, parity)
                    if k == SIDE - 2:
                        dve.wait_ge(side_read, index + 1)
                        dve.tensor_tensor(maxes[:, :, QT // 2:], maxes[:, :, QT // 2:], max_low[:, :, :],
                                          ALU.max).then_inc(max_ready, 1)

            def normalise(i, b, half):
                g = BATCH * i + b
                n = 2 * g + half
                dve.wait_ge(pv_done, NS * g + (NS if half else NS0))
                dve.transpose(turned[:, :], bank(6 + half)).then_inc(turn_done, 1)
                dve.wait_ge(turn_done, n + 1)
                t = turned[:, :].rearrange("p (k f) -> p k f", f=32)
                dve.reciprocal(recip[:, :], t[:, :, HD]).then_inc(recip_done, 1)
                dve.wait_ge(recip_done, n + 1)
                k = HALF // 32
                dst = Z[:, b, half * k:(half + 1) * k, bass.ds(i, 1), :].rearrange("p k o e -> p k (o e)")
                dve.tensor_tensor(dst, t[:, :, 0:HD], recip[:, :].unsqueeze(2).to_broadcast([P, k, HD]),
                                  ALU.mult).then_inc(z_done, 1)
                dve.wait_ge(z_done, n + 1)

            def group(i, b, last):
                for s in range(NS):
                    if not (last and b == 1):
                        side(i + b, 1 - b, s)
                    if s == 1 and not (isinstance(i, int) and i == 0 and b == 0):
                        normalise(i - 1 + b, 1 - b, 1)
                    if s == NS0 + 2:
                        normalise(i, b, 0)

            dve.wait_ge(causal_set, 1)
            for s in range(NS):
                side(0, 0, s)
            for b in range(BATCH):
                group(0, b, False)
            with dve.Fori(1, KVH - 1) as i:
                for b in range(BATCH):
                    group(i, b, False)
            for b in range(BATCH):
                group(KVH - 1, b, True)
            normalise(KVH - 1, 1, 1)
            for b in range(BATCH):
                for c in range(C):
                    dve.transpose(YT[:, c, b * SEQ:(b + 1) * SEQ],
                                  Z[:, b, :, 2 * c:2 * c + 2, :].rearrange("p k h e -> p k (h e)")).then_inc(yt_done, 1)

            dve.wait_ge(yt_done, 2 * C)
            for g in range(4):
                ts = range(4 * g, 4 * g + 4)
                for t in ts:
                    dve.wait_ge(wo_done, t + 1)
                    dve.tensor_tensor(X[:, t, :], X[:, t, :], bank(t % 4), ALU.add).then_inc(x1_done, 1)
                dve.wait_ge(x1_done, 4 * g + 4)
                for t in ts:
                    last = dve.bn_stats(stats[:, t, :], X[:, t, :])
                last.then_inc(ln2_stats, 1)
                dve.wait_ge(ln2_stats, g + 1)
                for t in ts:
                    last = dve.bn_aggr(mv[:, t, :], stats[:, t, :])
                last.then_inc(ln2_aggr, 1)
                dve.wait_ge(ln2_std, g + 1)
                dve.reciprocal(rstd[:, 4 * g:4 * g + 4], std[:, 4 * g:4 * g + 4]).then_inc(ln2_rstd, 1)
                dve.wait_ge(ln2_rstd, g + 1)
                if g:
                    dve.wait_ge(xn2_stored, 64 * g)
                    dve.wait_ge(turn2_done, 4 * g)
                for t in ts:
                    dve.tensor_scalar(xn2[:, t % 4, :], X[:, t, :], mv[:, t, 0:1], rstd[:, t:t + 1],
                                      ALU.subtract, ALU.mult).then_inc(xn2_ready, 1)

            steps = [0]

            def step(ins):
                steps[0] += 1
                ins.then_inc(route, 1)
                dve.wait_ge(route, steps[0])

            dve.wait_ge(logits_done, NT)
            dve.wait_ge(consts, 11)
            log = PS[:, 6 * BANK:8 * BANK].rearrange("p (t e) -> p t e", t=NT)
            all_te = [P, NT, E]
            step(dve.tensor_reduce(lmax[:, :], log, AXX, ALU.max))
            step(dve.tensor_tensor(tmp[:, :, :], log, lmax[:, :].unsqueeze(2).to_broadcast(all_te), ALU.subtract))
            step(dve.tensor_tensor(biased[:, :, :], log, bias_s[:, :].unsqueeze(1).to_broadcast(all_te), ALU.add))
            for t in range(NT):
                last = dve.max(top8[:, t, :], biased[:, t, :])
            step(last)
            for t in range(NT):
                last = dve.max_index(idx8[:, t, :], top8[:, t, :], biased[:, t, :])
            step(last)
            step(dve.tensor_copy(idxf[:, :, :], idx8[:, :, :]))
            dve.wait_ge(ex_ready, 1)
            for k in range(TOPK):
                step(dve.tensor_tensor(onehot[k][:, :, :], iota_e[:, :].unsqueeze(1).to_broadcast(all_te),
                                       idxf[:, :, k:k + 1].to_broadcast(all_te), ALU.is_equal))
                step(dve.tensor_tensor(tmp[:, :, :], onehot[k][:, :, :], ex[:, :, :], ALU.mult))
                step(dve.tensor_reduce(part_k[:, k, :], tmp[:, :, :], AXX, ALU.add))
                if k == 1:
                    step(dve.tensor_tensor(mask[:, :, :], onehot[0][:, :, :], onehot[1][:, :, :], ALU.add))
                if k > 1:
                    step(dve.tensor_tensor(mask[:, :, :], mask[:, :, :], onehot[k][:, :, :], ALU.add))
            step(dve.memset(cum[:, 0, :], 0.0))
            for t in range(1, NT):
                step(dve.tensor_tensor(cum[:, t, :], cum[:, t - 1, :], mask[:, t - 1, :], ALU.add))
            step(dve.tensor_tensor(total_b[:, :], cum[:, NT - 1, :], mask[:, NT - 1, :], ALU.add))
            dve.sem_inc(masks_ready, 1)
            step(dve.tensor_tensor(lmax[:, :], part_k[:, 0, :], part_k[:, 1, :], ALU.add))
            for k in range(2, TOPK):
                step(dve.tensor_tensor(lmax[:, :], lmax[:, :], part_k[:, k, :], ALU.add))
            step(dve.reciprocal(lmax[:, :], lmax[:, :]))
            step(dve.tensor_tensor(gates[:, :, :], part_k[:, :, :], lmax[:, :].unsqueeze(1).to_broadcast([P, TOPK, NT]),
                                   ALU.mult))
            dve.wait_ge(ranks_done, 1)
            step(dve.tensor_copy(counts[0:E, 0:1], bank(2, 1)[0:E, :]))
            step(dve.tensor_scalar(idxf[0:E, 0:2, :].rearrange("p a b -> p (a b)"), iota_c[0:E, :], counts[0:E, 0:1], None,
                                   ALU.is_lt))
            step(dve.tensor_reduce(counts[0:E, 1:2], idxf[0:E, 0:2, :].rearrange("p a b -> p (a b)"), AXX, ALU.add))
            step(dve.tensor_scalar(tiles_b[0:E, :], ones_b[0:E, :], counts[0:E, 1:2], None, ALU.mult))
            dve.sem_inc(tiles_ready, 1)
            dve.wait_ge(starts_done, 1)
            step(dve.tensor_copy(start_s[:, :], bank(3, E)))
            step(dve.tensor_scalar(top8[:, 0:8, :].rearrange("p a b -> p (a b)"), start_s[:, :], iota_p[:, 0:1], None,
                                   ALU.is_le))
            step(dve.tensor_reduce(counts[:, 2:3], top8[:, 0:8, :].rearrange("p a b -> p (a b)"), AXX, ALU.add))
            step(dve.tensor_scalar(counts[:, 4:5].bitcast(U32), counts[:, 2:3], -1.0, None, ALU.add))
            dve.sem_inc(experts_ready, 1)
            step(dve.tensor_scalar(start_s[:, :], start_s[:, :], float(P), None, ALU.mult))
            step(dve.tensor_tensor(pos[:, :, :], PS[:, 0:2 * BANK].rearrange("p (t e) -> p t e", t=NT),
                                   start_s[:, :].unsqueeze(1).to_broadcast(all_te), ALU.add))
            for k in range(TOPK):
                step(dve.tensor_tensor(tmp[:, :, :], onehot[k][:, :, :], pos[:, :, :], ALU.mult))
                step(dve.tensor_reduce(part_k[:, k, :], tmp[:, :, :], AXX, ALU.add))
            step(dve.tensor_copy(slot_u[:, :, :], part_k[:, :, :]))
            dve.sem_inc(slots_ready, 2)

            for g in range(4):
                if g:
                    dve.wait_ge(down_done, 4 * g)
                for n in range(HC * g, HC * (g + 1)):
                    dve.wait_ge(silu_done, n + 1)
                    dve.tensor_tensor(hidden[:, n % HC, :], silu_s[:, n % 2, :], bank(2 * (n % 2) + 1), ALU.mult)\
                       .then_inc(hidden_done, 1)
                for t in range(4 * g, 4 * g + 4):
                    dve.wait_ge(down_done, t + 1)
                    dve.tensor_tensor(X[:, t, :], X[:, t, :], bank(4 + t % 2), ALU.add).then_inc(shared_added, 1)

            dve.wait_ge(table_in, 16)
            dve.tensor_copy(tmp[:, 0:2, :].rearrange("p a b -> p (a b)"), tab[:, :]).then_inc(table_float, 1)
            dve.wait_ge(table_turned, 1)
            dve.tensor_copy(tab_t[:, :], bank(6, SLOT_TILES)).then_inc(table_ready, 1)

            def expert_hidden(n, k):
                dve.wait_ge(e_silu, n + 1)
                wait(dve, e_down, n - 1)
                dve.tensor_tensor(hg[:, k % 2, :], sg[:, k % 2, :], PS[:, (2 + k % 2) * BANK + F:(2 + k % 2) * BANK + 2 * F],
                                  ALU.mult).then_inc(e_hidden, 1)

            def expert_y(n, k, count):
                dve.wait_ge(e_down, n + 1)
                wait(dve, yb_stored[k % 2], 16 * count)
                dve.tensor_copy(yb[:, k % 2, :], bank(4 + k % 2)).then_inc(yb_ready, 1)

            def expert_tiles(i, first, last):
                for j in range(4):
                    n = 4 * i + j
                    expert_hidden(n, j)
                    if not (first and j == 0):
                        expert_y(n - 1, j - 1, 2 * i + (j - 1) // 2)

            expert_tiles(0, True, False)
            with dve.Fori(1, SLOT_TILES // 4 - 1) as i:
                expert_tiles(i, False, False)
            expert_tiles(SLOT_TILES // 4 - 1, False, True)
            expert_y(SLOT_TILES - 1, 3, SLOT_TILES // 2 - 1)

            for t in range(NT):
                dve.wait_ge(yk_in[t % 4], 16 * TOPK * (t // 4 + 1))
                for k in range(TOPK):
                    if k:
                        dve.wait_ge(mixed, TOPK * t + k)
                    dve.scalar_tensor_tensor(out=X[:, t, :], in0=yk[:, t % 4, k, :], scalar=gates[:, k, t:t + 1],
                                             in1=X[:, t, :], op0=ALU.mult, op1=ALU.add).then_inc(mixed, 1)


_INS = ['L0_attn_x', 'L0_attn_wq', 'L0_attn_wk', 'L0_attn_wv', 'L0_attn_wo', 'L0_ffn_router_w', 'L0_ffn_router_bias',
        'L0_ffn_wg', 'L0_ffn_wu', 'L0_ffn_wd', 'L0_ffn_swg', 'L0_ffn_swu', 'L0_ffn_swd']
_OUTS = [((BATCH, SEQ, D), 'float32')]


def kernel(**inputs):
    import numpy as _np
    import concourse.bacc as _bacc
    from concourse import mybir as _mybir
    from concourse.bass_utils import run_bass_kernel_spmd as _run

    nc = _bacc.Bacc("TRN2", target_bir_lowering=False, num_devices=1)
    arrays, args = {}, []
    for name in _INS:
        a = _np.ascontiguousarray(inputs[name])
        arrays[f"in_{name}_dram"] = a
        args.append(nc.dram_tensor(f"in_{name}_dram", a.shape, _mybir.dt.from_np(a.dtype), kind="ExternalInput").ap())
    for i, (shape, dtype) in enumerate(_OUTS):
        dt = _mybir.dt.from_np(_np.dtype(dtype))
        args.append(nc.dram_tensor(f"out_{i}_dram", shape, dt, kind="ExternalOutput").ap())
    build_block(nc, *args)
    r = _run(nc, [arrays], core_ids=[0])
    return r.results[0]["out_0_dram"]
```

```python
import concourse.bass as bass
from concourse import mybir
from contextlib import ExitStack

FP32 = mybir.dt.float32
BF16 = mybir.dt.bfloat16
U32 = mybir.dt.uint32
ACT = mybir.ActivationFunctionType
ALU = mybir.AluOpType
AXX = mybir.AxisListType.X

P = 128
BATCH, SEQ, D = 2, 1024, 512
NTOK = BATCH * SEQ
NT = NTOK // P
C = D // P
HEADS, KVH, HD = 32, 8, 16
REP = HEADS // KVH
QT = SEQ // P
BANK = 512
E, F, TOPK = 64, 128, 4
HID = 1024
HC = HID // P
SUB = P // 2
LANES = 8
LANE_TILES = -(-((TOPK * NTOK - E) // SUB + E) // LANES)
SLOTS = LANES * LANE_TILES * SUB
JP = LANES // 2
PAIRS = JP * LANE_TILES
EARLY = 3
YK = 3
EPS = 1e-5
NEG = -1e30

Q_PART = [0, 0, 1, 1, 0, 2]
K_PART = [0, 1, 0, 1, 2, 0]
STACK = len(Q_PART) * HD
KROWS = STACK + 2

HALF = SEQ // 2
WIN = SEQ // REP


def steps_of_half(half):
    full, odd = [], []
    for kt in range((half + 1) * HALF // P):
        q = max(kt * P, half * HALF)
        if q % WIN:
            odd.append((kt, q, P))
            q += P
        full += [[(kt, a, WIN, 0)] for a in range(q, (half + 1) * HALF, WIN)]
    pairs = [[(*odd[n], 0), (*odd[n + 1], REP * P)] for n in range(0, len(odd), 2)]
    return full + pairs


STEPS = steps_of_half(0) + steps_of_half(1)
NS = len(STEPS)
NS0 = len(steps_of_half(0))
PIECES = [(qt, lo, min(512, (qt + 1) * P - lo)) for qt in range(QT) for lo in range(0, (qt + 1) * P, 512)]
SIDE = REP * len(PIECES) + 1
LATE = 4
AHEAD = 16
MASKS = sum(x[0][1] == x[0][0] * P for x in STEPS)


def side_item(i, b, k):
    at, parity = SIDE * (BATCH * i + b) + k - 1, (SIDE * b + k - 1) % 2
    if k == LATE:
        return at, parity, (i - 1 + b, 1 - b), None
    return at, parity, (i, b), k - (k > LATE)


def side_items(i, b, last, s):
    found = []
    for k in range(AHEAD + s * SIDE // NS, AHEAD + (s + 1) * SIDE // NS):
        if k < SIDE and not (last and b == 1):
            found.append(side_item(i + b, 1 - b, k))
        elif k >= SIDE and not last:
            found.append(side_item(i + 1, b, k - SIDE))
        elif k == SIDE + LATE and b == 0:
            found.append((SIDE * BATCH * KVH - 1, 1, (i, 1), None))
    return found


FIRST_ITEMS = [(k, k % 2, (0, 0), k) for k in range(SIDE - 1)] + [side_item(0, 1, k) for k in range(AHEAD)]


def wait(eng, sem, value):
    if not (isinstance(value, int) and value <= 0):
        eng.wait_ge(sem, value)


def wait_alone(eng, sem, value, passed):
    eng.wait_ge(sem, value)
    eng.sem_inc(passed, 1)


def build_block(nc, x, wq, wk, wv, wo, router_w, router_bias, wg, wu, wd, swg, swu, swd, out):
    ctx = ExitStack()
    with ctx:
        def sb(name, shape, dt=FP32):
            return ctx.enter_context(nc.sbuf_tensor(name, shape, dt))

        def sem(name):
            return ctx.enter_context(nc.semaphore(name))

        def carve(arena, at, shape, dt=FP32):
            n = 1
            for d in shape[1:]:
                n *= d
            words = n * (2 if dt == BF16 else 4) // 4
            v = arena[0:shape[0], at:at + words]
            if dt != FP32:
                v = v.bitcast(dt)
            if len(shape) == 3:
                v = v.rearrange("p (a b) -> p a b", a=shape[1])
            if len(shape) == 4:
                v = v.rearrange("p (a b c) -> p a b c", a=shape[1], b=shape[2])
            return v, at + words

        def carve_all(arena, at, *wanted):
            views = []
            for shape, dt in wanted:
                v, at = carve(arena, at, shape, dt)
                views.append(v)
            return views

        qk_parts = nc.dram_tensor("qk_parts", [3, D + KVH * HD, NTOK], BF16)
        xn2_rows = nc.dram_tensor("xn2_rows", [NTOK, D], FP32)
        slot_tokens = nc.dram_tensor("slot_tokens", [SLOTS, 1], U32)
        slot_y = nc.dram_tensor("slot_y", [SLOTS, D], FP32)

        X = sb("X", [P, NT, D])
        XN = sb("XN", [P, NT, D])
        XT = sb("XT", [P, C, NTOK])
        att = sb("att", [P, 14336])
        w_att = sb("w_att", [P, 5120])
        ring = sb("ring", [P, 4 * 3 * C * F])
        small = sb("small", [P, 1536])
        ident = sb("ident", [P, P])
        eps_s = sb("eps_s", [P, 1])
        stats = sb("stats", [P, NT, 6])
        mv = sb("mv", [P, NT, 2])
        std = sb("std", [P, NT])
        rstd = sb("rstd", [P, NT])
        v_head = [sb(f"v_head{b}", [P, QT, 2 * HD]) for b in range(BATCH)]
        maxes = [sb(f"maxes{b}", [P, REP, QT]) for b in range(BATCH)]
        max_low = sb("max_low", [P, REP, QT // 2])
        max_rows = sb("max_rows", [REP * QT, 2, P], BF16)
        recip = sb("recip", [P, HALF // 32])
        router_s = sb("router_s", [P, C, E])
        bias_s = sb("bias_s", [P, E])

        wq_s, wk_s, wv_s, wo_s = carve_all(w_att, 0, ([P, C, D], FP32), ([P, C, KVH * HD], FP32),
                                           ([P, C, KVH * HD], FP32), ([P, C, D], FP32))
        v_all = carve(ring, 0, [P, NT, KVH * HD])[0].rearrange("p t (k d) -> p t k d", k=KVH)
        probs, *stacks = carve_all(att, 0, ([P, 4, REP * WIN], FP32), *[([P, REP, SEQ], BF16)] * 4,
                                   *[([P, SEQ], BF16)] * 4)
        q_max, q_exp, k_max, k_exp = stacks[0:2], stacks[2:4], stacks[4:6], stacks[6:8]
        stage, rest = carve_all(att, 0, ([P, 2, 3 * BANK], BF16), ([P, BANK], FP32))
        stage = stage.rearrange("p n (a t) -> p n a t", a=3)
        turned, causal, junk = carve_all(small, 0, ([P, HALF], FP32), ([P, BANK], FP32), ([P, 2, BANK], BF16))
        Z = XN[:, :, :].rearrange("p n d -> p (n d)").rearrange("p (b k h e) -> p b k h e", b=BATCH, h=KVH, e=HD)
        YT = XT

        flat_xn = XN[:, :, :].rearrange("p n d -> p (n d)")
        flat_xt = XT[:, :, :].rearrange("p c t -> p (c t)")
        XT2 = flat_xn.rearrange("p (c t) -> p c t", c=C)
        xn2, = carve_all(w_att, 0, ([P, 4, D], FP32))
        swg_s, swu_s, swd_s, tmp, mask, cum = carve_all(
            att, 0, ([P, 2 * C, D], FP32), ([P, 2 * C, D], FP32), ([P, HC, D], FP32), ([P, NT, E], FP32),
            ([P, NT, E], BF16), ([P, NT, E], BF16))
        hidden, biased, ex, *onehot = carve_all(
            flat_xt, 0, ([P, HC, BANK], FP32), ([P, NT, E], FP32), ([P, NT, E], FP32), *[([P, NT, E], BF16)] * TOPK)
        pos = biased
        row_e = carve(att, 13312, [1, LANES * LANE_TILES], U32)[0]
        silu_s, = carve_all(w_att, 4096, ([P, 2, BANK], FP32))
        (tri, ones_b, iota_e, top8, idx8, idxf, part_k, gates, slot_u, tab, tab_t, lmax, counts, start_s, tile_no,
         total_b, tiles_b, iota_c, token_ids, found, code) = carve_all(
            small, 0, ([P, P], BF16), ([P, P], BF16), ([P, E], FP32), ([P, NT, 8], FP32), ([P, NT, 8], U32),
            ([P, NT, 8], FP32), ([P, TOPK, NT], FP32), ([P, TOPK, NT], FP32), ([P, TOPK, NT], U32),
            ([P, P], U32), ([P, PAIRS], U32), ([P, NT], FP32), ([P, 2], FP32), ([P, E], FP32),
            ([P, 2 * LANES], FP32), ([P, E], BF16), ([P, P], BF16), ([P, NTOK // SUB], FP32), ([P, NT], U32),
            ([P, 2 * LANES], FP32), ([P, LANES], U32))
        lane_w = [carve(ring, n * 3 * C * F, [P, 3, C * F])[0] for n in range(4)]
        lane_w += [carve(flat_xt, n * 3 * C * F, [P, 3, C * F])[0] for n in range(4)]
        xg, xgt, yb, sg, ht, hg = carve_all(w_att, 0, ([P, 4, D], FP32), ([P, 2, D], FP32), ([P, 2, D], FP32),
                                            ([P, 2, P], FP32), ([P, 2, P], FP32), ([P, 2, P], FP32))
        idx = sb("idx", [P, 4], U32)
        yk = carve(ring, 0, [P, YK, TOPK, D])[0]

        PS = ctx.enter_context(nc.psum_tensor("PS", [P, 8 * BANK], FP32))

        def bank(k, n=BANK):
            return PS[:, k * BANK:k * BANK + n]

        x_in = [sem(f"x_in{g}") for g in range(4)]
        w_in = sem("w_in")
        pool_passed = sem("pool_passed")
        dve_passed = sem("dve_passed")
        eps_set = sem("eps_set")
        ident_zero = sem("ident_zero")
        ident_set = sem("ident_set")
        causal_zero = sem("causal_zero")
        causal_set = sem("causal_set")
        v_ones = sem("v_ones")
        k_ones = sem("k_ones")
        ln_stats = sem("ln_stats")
        ln_aggr = sem("ln_aggr")
        ln_std = sem("ln_std")
        ln_rstd = sem("ln_rstd")
        xn_ready = sem("xn_ready")
        prep_done = sem("prep_done")
        prep_read = [sem(f"prep_read{k}") for k in range(8)]
        xt_ready = [sem("xt_ready_dve"), sem("xt_ready_act")]
        part_hi = sem("part_hi")
        part_rest = sem("part_rest")
        part_mid = sem("part_mid")
        part_low = sem("part_low")
        parts_out = [sem("parts_out0"), sem("parts_out1")]
        v_done = sem("v_done")

        max_in = [sem("max_in0"), sem("max_in1")]
        exp_in = [sem("exp_in0"), sem("exp_in1")]
        v_in = [sem("v_in0"), sem("v_in1")]
        side_done = sem("side_done")
        side_read = sem("side_read")
        reduced = sem("reduced")
        max_ready = sem("max_ready")
        max_hi = sem("max_hi")
        rows_ready = sem("rows_ready")
        rows_in = sem("rows_in")
        scores_done = sem("scores_done")
        exp_done = sem("exp_done")
        masked = sem("masked")
        pv_done = sem("pv_done")
        turn_done = sem("turn_done")
        recip_done = sem("recip_done")
        z_done = sem("z_done")
        yt_done = sem("yt_done")

        shared_in = sem("shared_in")
        x1_done = sem("x1_done")
        ln2_stats = sem("ln2_stats")
        ln2_aggr = sem("ln2_aggr")
        ln2_std = sem("ln2_std")
        ln2_rstd = sem("ln2_rstd")
        wo_done = sem("wo_done")
        xn2_ready = sem("xn2_ready")
        xn2_stored = sem("xn2_stored")
        turn2_done = sem("turn2_done")
        xt2_ready = sem("xt2_ready")
        logits_done = sem("logits_done")
        consts = sem("consts")
        route = sem("route")
        ex_ready = sem("ex_ready")
        masks_ready = sem("masks_ready")
        ranks_done = sem("ranks_done")
        tiles_ready = sem("tiles_ready")
        starts_done = sem("starts_done")
        slots_ready = sem("slots_ready")
        table_zero = sem("table_zero")
        table_set = sem("table_set")
        table_in = sem("table_in")
        table_float = sem("table_float")
        table_turned = sem("table_turned")
        table_ready = sem("table_ready")
        experts_ready = sem("experts_ready")
        experts_in = sem("experts_in")
        up_done = sem("up_done")
        silu_done = sem("silu_done")
        hidden_done = sem("hidden_done")
        down_done = sem("down_done")
        shared_added = sem("shared_added")

        lane_up_in = [sem(f"lane_up_in{n}") for n in range(LANES)]
        lane_down_in = [sem(f"lane_down_in{n}") for n in range(LANES)]
        idx_set = sem("idx_set")
        xg_in = [sem(f"xg_in{j}") for j in range(4)]
        xg_turned = sem("xg_turned")
        xgt_ready = sem("xgt_ready")
        e_up = sem("e_up")
        e_silu = sem("e_silu")
        e_hidden = sem("e_hidden")
        e_turn = sem("e_turn")
        e_turned = sem("e_turned")
        e_down = sem("e_down")
        yb_ready = sem("yb_ready")
        yb_stored = [sem("yb_stored0"), sem("yb_stored1")]
        yk_in = [sem(f"yk_in{n}") for n in range(YK)]
        mixed = sem("mixed")
        stored = sem("stored")

        x_view = x.rearrange("b (n p) d -> p (b n) d", p=P)
        out_view = out.rearrange("b (n p) d -> p (b n) d", p=P)

        jobs = [("T", t) for t in range(4)]
        for g in range(4):
            jobs += [("T", t) for t in range(4 * g + 4, min(4 * g + 8, NT))]
            jobs += [("QK", (m, g)) for m in range(C + 1)] + [("V", g)]
        QK_JOBS = (C + 1) * 4

        block = ctx.enter_context(nc.Block())

        @block.sync
        def _(sp):
            for g in range(4):
                sp.dma_start(X[:, 4 * g:4 * g + 4, :], x_view[:, 4 * g:4 * g + 4, :]).then_inc(x_in[g], 16)
            for n, (m, g) in enumerate([a for k, a in jobs if k == "QK"]):
                sp.wait_ge(part_low, n + 1)
                sp.dma_start(qk_parts[:, m * P:(m + 1) * P, g * BANK:(g + 1) * BANK].rearrange("a p t -> p a t"),
                             stage[:, n % 2, :, :]).then_inc(parts_out[n % 2], 16)
            for s in parts_out:
                sp.wait_ge(s, 16 * QK_JOBS // 2)

            def load_stack(q, k, i, b, done):
                at = slice(b * SEQ, (b + 1) * SEQ)
                for j in range(len(Q_PART)):
                    sp.dma_start(q[b][j * HD:(j + 1) * HD, :, :],
                                 qk_parts[Q_PART[j], bass.ds(i * (REP * HD), REP * HD), at]
                                 .rearrange("(r d) t -> d r t", r=REP)).then_inc(done[b], 16)
                    sp.dma_start(k[b][j * HD:(j + 1) * HD, :],
                                 qk_parts[K_PART[j], bass.ds(i * HD + D, HD), at]).then_inc(done[b], 16)

            def group(i, b, last):
                g = BATCH * i + b
                if not last:
                    sp.wait_ge(side_done, SIDE * g + SIDE - 1)
                    load_stack(q_max, k_max, i + 1, b, max_in)
                if not (last and b == BATCH - 1):
                    sp.wait_ge(rows_ready, g + 2)
                    for h in range(2):
                        sp.dma_start(q_exp[1 - b][STACK + h:STACK + h + 1, :, :], max_rows[:, h, :])\
                          .then_inc(rows_in, 16)
                if not last:
                    sp.wait_ge(scores_done, NS * (g + 1))
                    load_stack(q_exp, k_exp, i + 1, b, exp_in)

            for b in range(BATCH):
                load_stack(q_max, k_max, 0, b, max_in)
                load_stack(q_exp, k_exp, 0, b, exp_in)
            sp.wait_ge(rows_ready, 1)
            for h in range(2):
                sp.dma_start(q_exp[0][STACK + h:STACK + h + 1, :, :], max_rows[:, h, :]).then_inc(rows_in, 16)
            for b in range(BATCH):
                group(0, b, False)
            with sp.Fori(1, KVH - 1) as i:
                for b in range(BATCH):
                    group(i, b, False)
            for b in range(BATCH):
                group(KVH - 1, b, True)
            sp.wait_ge(z_done, 4 * KVH)
            for dst, src in ((swg_s, swg), (swu_s, swu)):
                sp.dma_start(dst.rearrange("p (s c) n -> p s c n", s=2), src.rearrange("s (c p) n -> p s c n", p=P))\
                  .then_inc(shared_in, 16)
            sp.dma_start(swd_s.rearrange("p (s c) n -> p s c n", s=2), swd.rearrange("s (c p) n -> p s c n", p=P))\
              .then_inc(shared_in, 16)
            for t in range(NT):
                sp.wait_ge(xn2_ready, t + 1)
                sp.dma_start(xn2_rows[t * P:(t + 1) * P, :], xn2[:, t % 4, :]).then_inc(xn2_stored, 16)
            sp.wait_ge(experts_ready, 1)
            sp.dma_start(row_e[0:1, :], code[0:LANE_TILES, :]).then_inc(experts_in, 16)
            sp.wait_ge(table_set, 16 * TOPK * NT)
            for n in range(LANES):
                j, l = n // 2, n % 2
                sp.dma_start(tab[j * LANE_TILES:(j + 1) * LANE_TILES, l * SUB:(l + 1) * SUB],
                             slot_tokens[n * LANE_TILES * SUB:(n + 1) * LANE_TILES * SUB, :]
                             .rearrange("(i q) o -> i (q o)", q=SUB)).then_inc(table_in, 16)

            def load_up(i, j):
                codes = []
                for n in (2 * j, 2 * j + 1):
                    code = sp.value_load(row_e[0:1, bass.ds(i * LANES + n, 1)], min_val=0, max_val=2 * E - 1)
                    e, new = sp.snap(code % E, min_val=0, max_val=E - 1), sp.snap(code // E, min_val=0, max_val=1)
                    codes.append((e, new))
                    wait(sp, e_up, JP * (i - 1) + j + 1)
                    for k, w in enumerate((wg, wu)):
                        sp.dma_start(lane_w[n][:, k, :], w[bass.ds(e, 1), :, :].rearrange("o (p c) f -> p (o c f)", c=C),
                                     cond=new).then_inc(lane_up_in[n], 16)
                return codes

            def load_down(i, j, codes):
                for n, (e, new) in zip((2 * j, 2 * j + 1), codes):
                    wait(sp, e_down, JP * (i - 1) + j + 1)
                    sp.dma_start(lane_w[n][:, 2, :], wd[bass.ds(e, 1), :, :].rearrange("o f d -> f (o d)"),
                                 cond=new).then_inc(lane_down_in[n], 16)

            def load_pairs(i, first):
                codes = []
                for j in range(JP):
                    if first and j == 2:
                        sp.wait_ge(down_done, 4 * EARLY)
                    codes.append(load_up(i, j))
                    if j:
                        load_down(i, j - 1, codes[j - 1])
                load_down(i, JP - 1, codes[JP - 1])

            sp.wait_ge(experts_in, 16)
            load_pairs(0, True)
            with sp.Fori(1, LANE_TILES) as i:
                load_pairs(i, False)
            for t in range(NT):
                sp.wait_ge(mixed, TOPK * (t + 1))
                sp.dma_start(out_view[:, t, :], X[:, t, :]).then_inc(stored, 16)
            sp.wait_ge(stored, 16 * NT)

        @block.gpsimd
        def _(pool):
            pool.memset(eps_s[:, :], EPS).then_inc(eps_set, 1)
            pool.memset(ident[:, :], 0.0).then_inc(ident_zero, 1)
            pool.wait_ge(ident_zero, 1)
            pool.affine_select(out=ident[:, :], in_=ident[:, :], compare_op=ALU.not_equal, fill=1.0, base=0,
                               pattern=[[-1, P]], channel_multiplier=1).then_inc(ident_set, 1)
            for b in range(BATCH):
                pool.memset(v_head[b][:, :, :], 1.0).then_inc(v_ones, 1)
            pool.memset(causal[:, :], 0.0).then_inc(causal_zero, 1)
            pool.wait_ge(causal_zero, 1)
            pool.affine_select(out=causal[:, BANK - P:], in_=causal[:, BANK - P:], compare_op=ALU.is_ge, fill=NEG,
                               base=0, pattern=[[-1, P]], channel_multiplier=1).then_inc(causal_set, 1)
            pool.wait_ge(causal_set, 1)
            for b in range(BATCH):
                pool.memset(k_exp[b][STACK:KROWS, :], 1.0).then_inc(k_ones, 1)
                pool.wait_ge(k_ones, b + 1)

            def load_v(i, b):
                pool.tensor_copy(v_head[b][:, :, 0:HD], v_all[:, b * QT:(b + 1) * QT, bass.ds(i, 1), :]
                                 .rearrange("p t o e -> p t (o e)")).then_inc(v_in[b], 1)

            def group(i, b, last):
                g = BATCH * i + b
                for s, segments in enumerate(STEPS):
                    if s == 3 and not (last and b == 1):
                        wait(pool, pv_done, NS * g)
                        load_v(i + b, 1 - b)
                    if segments[0][1] - segments[0][0] * P not in (0,):
                        continue
                    wait_alone(pool, exp_done, NS * g + s + 1, pool_passed)
                    n = len(segments) * REP
                    d = probs[:, (NS * b + s) % 4, :].rearrange("p (r q) -> p r q", r=n)[:, :, 0:P]
                    pool.affine_select(out=d, in_=d, compare_op=ALU.is_ge, fill=0.0, base=0,
                                       pattern=[[0, n], [1, P]], channel_multiplier=-1).then_inc(masked, 1)

            pool.wait_ge(v_done, 4)
            pool.wait_ge(v_ones, 2)
            load_v(0, 0)
            for b in range(BATCH):
                group(0, b, False)
            with pool.Fori(1, KVH - 1) as i:
                for b in range(BATCH):
                    group(i, b, False)
            for b in range(BATCH):
                group(KVH - 1, b, True)

            pool.wait_ge(z_done, 4 * KVH)
            pool.wait_ge(side_read, SIDE * BATCH * KVH)
            pool.memset(ones_b[:, :], 1.0).then_inc(consts, 1)
            pool.memset(tri[:, :], 1.0).then_inc(consts, 1)
            pool.wait_ge(consts, 2)
            pool.affine_select(out=tri[:, :], in_=tri[:, :], compare_op=ALU.is_gt, fill=0.0, base=0,
                               pattern=[[1, P]], channel_multiplier=-1).then_inc(consts, 1)
            pool.iota(top8[:, 0:8, :].rearrange("p a b -> p (a b)").bitcast(U32), pattern=[[1, E]], base=0,
                      channel_multiplier=0).then_inc(consts, 1)
            for h in range(2):
                pool.iota(top8[:, 8 + h, :].bitcast(U32), pattern=[[LANE_TILES, LANES]], base=-h,
                          channel_multiplier=1).then_inc(consts, 1)
            pool.iota(idxf[:, 0:4, :].rearrange("p a b -> p (a b)").bitcast(U32), pattern=[[SUB, NTOK // SUB]], base=0,
                      channel_multiplier=0).then_inc(consts, 1)
            pool.iota(token_ids[:, :], pattern=[[P, NT]], base=0, channel_multiplier=1).then_inc(consts, 1)
            pool.memset(tab[:, :], 0).then_inc(consts, 1)
            pool.wait_ge(consts, 9)
            pool.tensor_copy(iota_e[:, :], top8[:, 0:8, :].rearrange("p a b -> p (a b)").bitcast(U32)).then_inc(consts, 1)
            pool.tensor_copy(tile_no[:, :], top8[:, 8:10, :].rearrange("p a b -> p (a b)").bitcast(U32)).then_inc(consts, 1)
            pool.tensor_copy(iota_c[:, :], idxf[:, 0:4, :].rearrange("p a b -> p (a b)").bitcast(U32)).then_inc(consts, 1)
            pool.wait_ge(consts, 12)
            pool.affine_select(out=tile_no[:, LANES:], in_=tile_no[:, LANES:], compare_op=ALU.is_gt, fill=-1.0, base=0,
                               pattern=[[0, LANES]], channel_multiplier=1).then_inc(consts, 1)
            pool.dma_start(slot_tokens.rearrange("(s p) o -> s (p o)", p=P), tab[0:PAIRS, :]).then_inc(table_zero, 16)
            pool.wait_ge(table_zero, 16)
            pool.wait_ge(slots_ready, 1)
            for k in range(TOPK):
                for t in range(NT):
                    pool.indirect_dma_start(out=slot_tokens[:, :],
                                            out_offset=bass.IndirectOffsetOnAxis(ap=slot_u[:, k, t:t + 1], axis=0),
                                            in_=token_ids[:, t:t + 1], in_offset=None).then_inc(table_set, 16)

            def gather_tokens(i, j):
                n = JP * i + j
                wait(pool, xg_turned, n - 3)
                pool.tensor_copy(idx[:, j:j + 1], tab_t[:, bass.ds(j * LANE_TILES + i, 1)]).then_inc(idx_set, 1)
                wait_alone(pool, idx_set, n + 1, pool_passed)
                pool.indirect_dma_start(out=xg[:, j, :], out_offset=None, in_=xn2_rows[:, :],
                                        in_offset=bass.IndirectOffsetOnAxis(ap=idx[:, j:j + 1], axis=0))\
                    .then_inc(xg_in[j], 16)

            pool.wait_ge(table_ready, 1)
            pool.wait_ge(xn2_stored, 16 * NT)
            for j in range(JP):
                gather_tokens(0, j)
            with pool.Fori(1, LANE_TILES) as i:
                for j in range(JP):
                    gather_tokens(i, j)
            for s in yb_stored:
                pool.wait_ge(s, 16 * PAIRS)
            for t in range(NT):
                if t >= YK:
                    pool.wait_ge(mixed, TOPK * (t - YK + 1))
                for k in range(TOPK):
                    pool.indirect_dma_start(out=yk[:, t % YK, k, :], out_offset=None, in_=slot_y[:, :],
                                            in_offset=bass.IndirectOffsetOnAxis(ap=slot_u[:, k, t:t + 1], axis=0))\
                        .then_inc(yk_in[t % YK], 16)

        @block.scalar
        def _(act):
            for dst, src in ((wk_s, wk), (wv_s, wv), (wq_s, wq), (wo_s, wo)):
                if dst is not wo_s:
                    act.dma_start(dst[:, :, :], src.rearrange("(c p) n -> p c n", p=P)).then_inc(w_in, 16)
            wo_rows = wo.rearrange("(c k r d) n -> r k d c n", k=2, r=REP, d=HD)
            for r in range(REP):
                for k in range(2):
                    at = (2 * r + k) * HD
                    act.dma_start(wo_s[at:at + HD, :, :], wo_rows[r, k]).then_inc(w_in, 16)
            act.dma_start(router_s[:, :, :], router_w.rearrange("(c p) e -> p c e", p=P)).then_inc(w_in, 16)
            act.dma_start(bias_s[:, :], router_bias.partition_broadcast(P)).then_inc(w_in, 16)
            act.wait_ge(eps_set, 1)

            def deviation(g):
                act.wait_ge(ln_aggr, g + 1)
                act.activation(std[:, 4 * g:4 * g + 4], mv[:, 4 * g:4 * g + 4, 1], ACT.Sqrt, bias=eps_s[:, :])\
                   .then_inc(ln_std, 1)

            deviation(0)
            qk = 0
            for j, (kind, a) in enumerate(jobs):
                if kind == "T" and a % 4 == 0 and a + 4 < NT:
                    deviation(a // 4 + 1)
                if kind == "T" and a % 2 == 1:
                    act.wait_ge(prep_done, j + 1)
                    act.activation(XT[:, :, a * P:(a + 1) * P], bank(j % 8).rearrange("p (c t) -> p c t", c=C),
                                   ACT.Copy).then_inc(xt_ready[1], 1)
                    pass
                if kind == "QK":
                    act.wait_ge(prep_done, j + 1)
                    if qk >= 2:
                        act.wait_ge(parts_out[qk % 2], 16 * (qk // 2))
                    act.activation(stage[:, qk % 2, 0, :], bank(j % 8), ACT.Copy).then_inc(part_hi, 1)
                    qk += 1

            def exps(i):
                for n0 in range(BATCH * NS):
                    n = BATCH * NS * i + n0
                    act.wait_ge(scores_done, n + 1)
                    wait(act, pv_done, n - 3)
                    act.activation(probs[:, n0 % 4, :], PS[:, (n0 % 2) * 2 * BANK:(n0 % 2 + 1) * 2 * BANK], ACT.Exp,
                                   scale=HD ** -0.5).then_inc(exp_done, 1)

            exps(0)
            with act.Fori(1, KVH - 1) as i:
                exps(i)
            exps(KVH - 1)

            for g in range(4):
                act.wait_ge(ln2_aggr, g + 1)
                act.activation(std[:, 4 * g:4 * g + 4], mv[:, 4 * g:4 * g + 4, 1], ACT.Sqrt, bias=eps_s[:, :])\
                   .then_inc(ln2_std, 1)
                for t in range(4 * g, 4 * g + 4):
                    act.wait_ge(turn2_done, t + 1)
                    act.activation(XT2[:, :, t * P:(t + 1) * P], bank(4 + t % 2).rearrange("p (c t) -> p c t", c=C),
                                   ACT.Copy).then_inc(xt2_ready, 1)
            act.wait_ge(route, 2)
            act.activation(ex[:, :, :], tmp[:, :, :], ACT.Exp).then_inc(ex_ready, 1)
            def shared_silu(g):
                for n in range(HC * g, HC * (g + 1)):
                    act.wait_ge(up_done, n + 1)
                    if n >= 2:
                        act.wait_ge(hidden_done, n - 1)
                    act.activation(silu_s[:, n % 2, :], bank(2 * (n % 2)), ACT.Silu).then_inc(silu_done, 1)

            for g in range(EARLY):
                shared_silu(g)

            def turned_tokens(n, k):
                act.wait_ge(xg_turned, n + 1)
                wait(act, e_up, n - 1)
                act.activation(xgt[:, k % 2, :], bank(k % 2), ACT.Copy).then_inc(xgt_ready, 1)

            def silu(n, k):
                act.wait_ge(e_up, n + 1)
                wait(act, e_hidden, n - 1)
                act.activation(sg[:, k % 2, :], bank(2 + k % 2, F), ACT.Silu).then_inc(e_silu, 1)

            def store_y(i, j):
                act.wait_ge(yb_ready, JP * i + j + 1)
                rows = slot_y.rearrange("(j l i q) d -> j l i q d", l=2, i=LANE_TILES, q=SUB)
                for l in range(2):
                    act.dma_start(rows[j, l, bass.ds(i, 1), :, :].rearrange("o q d -> (o q) d"),
                                  yb[l * SUB:(l + 1) * SUB, j % 2, :]).then_inc(yb_stored[j % 2], 16)

            def expert_pairs(i, first, last):
                for j in range(JP):
                    n = JP * i + j
                    if not (last and j == JP - 1):
                        turned_tokens(n + 1, j + 1)
                    silu(n, j)
                    if not (first and j < 3):
                        store_y(i if j == 3 else i - 1, (j + 1) % JP if j < 3 else 0)

            turned_tokens(0, 0)
            expert_pairs(0, True, False)
            with act.Fori(1, LANE_TILES - 1) as i:
                expert_pairs(i, False, False)
            expert_pairs(LANE_TILES - 1, False, True)
            for j in range(1, JP):
                store_y(LANE_TILES - 1, j)
            act.wait_ge(e_down, PAIRS)
            act.wait_ge(e_hidden, PAIRS)
            for g in range(EARLY, 4):
                shared_silu(g)
            for s in yb_stored:
                act.wait_ge(s, 16 * PAIRS)

        @block.tensor
        def _(pe):
            pe.wait_ge(ident_set, 1)
            seen = {}
            for j, (kind, a) in enumerate(jobs):
                if j >= 8:
                    pk, pa = jobs[j - 8]
                    if pk == "T":
                        pe.wait_ge(xt_ready[pa % 2], pa // 2 + 1)
                    elif pk == "QK":
                        pe.wait_ge(part_rest, seen[j - 8] + 1)
                    else:
                        pe.wait_ge(v_done, pa + 1)
                if kind == "T":
                    pe.wait_ge(xn_ready, a + 1)
                    for c in range(C):
                        mm = pe.transpose(PS[:, (j % 8) * BANK + c * P:(j % 8) * BANK + (c + 1) * P],
                                          XN[:, a, c * P:(c + 1) * P], ident[:, :])
                elif kind == "QK":
                    m, g = a
                    seen[j] = (C + 1) * g + m
                    if m == 0:
                        pe.wait_ge(w_in, 16 * 13)
                        for s in xt_ready:
                            pe.wait_ge(s, 2 * g + 2)
                    for c in range(C):
                        w = wq_s[:, c, m * P:(m + 1) * P] if m < C else wk_s[:, c, :]
                        mm = pe.matmul(bank(j % 8), w, XT[:, c, g * BANK:(g + 1) * BANK],
                                       start=(c == 0), stop=(c == C - 1))
                else:
                    for t in range(4):
                        for c in range(C):
                            mm = pe.matmul(PS[:, (j % 8) * BANK + t * P:(j % 8) * BANK + (t + 1) * P],
                                           XT[:, c, (4 * a + t) * P:(4 * a + t + 1) * P], wv_s[:, c, :],
                                           start=(c == 0), stop=(c == C - 1))
                mm.then_inc(prep_done, 1)

            def piece(b, k, index, parity):
                wait(pe, side_read, index - 1)
                qt, lo, n = PIECES[k % len(PIECES)]
                pe.matmul(bank(4 + parity % 2, n), q_max[b][0:STACK, k // len(PIECES), qt * P:(qt + 1) * P],
                          k_max[b][0:STACK, lo:lo + n], start=True, stop=True).then_inc(side_done, 1)

            def turn(g, b, index, parity):
                pe.wait_ge(max_ready, g + 1)
                wait(pe, side_read, index - 1)
                pe.transpose(bank(4 + parity % 2, P)[0:REP * QT, :], maxes[b][:, :, :].rearrange("p r t -> p (r t)"),
                             ident[:, :]).then_inc(side_done, 1)

            def side(index, parity, group, k):
                i, b = group
                if k == 0:
                    pe.wait_ge(max_in[b], 16 * 2 * len(Q_PART) * (i + 1))
                if k is None:
                    turn(BATCH * i + b, b, index, parity)
                else:
                    piece(b, k, index, parity)

            def scores(i, b, s, between=()):
                n, parity = NS * (BATCH * i + b) + s, (NS * b + s) % 2
                if s == 0:
                    pe.wait_ge(exp_in[b], 16 * 2 * len(Q_PART) * (i + 1))
                    pe.wait_ge(rows_in, 32 * (BATCH * i + b + 1))
                wait(pe, exp_done, n - 1)
                for kt, q0, qn, col in STEPS[s]:
                    rows = BANK // qn
                    for r in range(0, REP, rows):
                        if (kt, r) != (STEPS[s][0][0], 0):
                            for item in between:
                                side(*item)
                        at = parity * 2 * BANK + col + r * qn
                        mm = pe.matmul(PS[:, at:at + BANK], k_exp[b][0:KROWS, kt * P:(kt + 1) * P],
                                       q_exp[b][0:KROWS, r:r + rows, q0:q0 + qn], start=True, stop=True)
                mm.then_inc(scores_done, 1)

            def values(i, b, s):
                g = BATCH * i + b
                n = NS * g + s
                pe.wait_ge(exp_done, n + 1)
                if s == 0:
                    pe.wait_ge(v_in[b], i + 1)
                    wait(pe, turn_done, 2 * g - 1)
                if s == NS0:
                    wait(pe, turn_done, 2 * g)
                if STEPS[s][0][1] == STEPS[s][0][0] * P:
                    pe.wait_ge(masked, MASKS * g + sum(x[0][1] == x[0][0] * P for x in STEPS[:s + 1]))
                for kt, q0, qn, col in STEPS[s]:
                    for r in range(REP):
                        at = 6 * BANK + q0
                        a = col + r * qn
                        mm = pe.matmul(PS[32 * r:32 * r + 32, at:at + qn], v_head[b][:, kt, :],
                                       probs[:, (NS * b + s) % 4, a:a + qn], start=s in (0, NS0), stop=False,
                                       skip_group_check=True)
                mm.then_inc(pv_done, 1)

            def group(i, b, last):
                for s in range(NS):
                    items = side_items(i, b, last, s)
                    for item in items[:1]:
                        side(*item)
                    if s + 1 < NS:
                        scores(i, b, s + 1, items[1:2])
                    elif not (last and b == 1):
                        scores(i + b, 1 - b, 0, items[1:2])
                    for item in items[2:]:
                        side(*item)
                    if s > 0:
                        values(i, b, s - 1)
                    elif not (isinstance(i, int) and i == 0 and b == 0):
                        values(i - 1 + b, 1 - b, NS - 1)

            pe.wait_ge(k_ones, 2)
            pe.wait_ge(v_done, 4)
            pe.wait_ge(part_rest, QK_JOBS)
            for item in FIRST_ITEMS:
                side(*item)
            scores(0, 0, 0)
            for b in range(BATCH):
                group(0, b, False)
            with pe.Fori(1, KVH - 1) as i:
                for b in range(BATCH):
                    group(i, b, False)
            for b in range(BATCH):
                group(KVH - 1, b, True)
            values(KVH - 1, 1, NS - 1)

            def project(t):
                pe.wait_ge(yt_done, C * (t // QT + 1))
                if t == 0:
                    pe.wait_ge(exp_done, NS * BATCH * KVH)
                if t >= 4:
                    pe.wait_ge(x1_done, t - 3)
                for c in range(C):
                    mm = pe.matmul(bank(t % 4), YT[:, c, t * P:(t + 1) * P], wo_s[:, c, :],
                                   start=(c == 0), stop=(c == C - 1))
                mm.then_inc(wo_done, 1)

            def turn_tokens(t):
                pe.wait_ge(xn2_ready, t + 1)
                if t >= 2:
                    pe.wait_ge(xt2_ready, t - 1)
                for c in range(C):
                    mm = pe.transpose(PS[:, (4 + t % 2) * BANK + c * P:(4 + t % 2) * BANK + (c + 1) * P],
                                      xn2[:, t % 4, c * P:(c + 1) * P], ident[:, :])
                mm.then_inc(turn2_done, 1)

            def logits(t):
                pe.wait_ge(xt2_ready, t + 1)
                at = 6 * BANK + t * E
                for c in range(C):
                    mm = pe.matmul(PS[:, at:at + E], XT2[:, c, t * P:(t + 1) * P], router_s[:, c, :],
                                   start=(c == 0), stop=(c == C - 1))
                mm.then_inc(logits_done, 1)

            for g in range(5):
                if g < 4:
                    for t in range(4 * g, 4 * g + 4):
                        project(t)
                if g >= 1:
                    for t in range(4 * g - 4, 4 * g):
                        turn_tokens(t)
                    for t in range(4 * g - 4, 4 * g):
                        logits(t)

            pe.wait_ge(masks_ready, 1)
            for h in range(2):
                half = slice(h * NT // 2, (h + 1) * NT // 2)
                flat = lambda v: v[:, half, :].rearrange("p t e -> p (t e)")
                pe.matmul(bank(h), tri[:, :], flat(mask), start=True, stop=False)
                pe.matmul(bank(h), ones_b[:, :], flat(cum), start=False, stop=True)
            pe.matmul(bank(2, 1)[0:E, :], total_b[:, :], ones_b[:, 0:1], start=True, stop=True).then_inc(ranks_done, 1)
            pe.wait_ge(tiles_ready, 1)
            pe.matmul(bank(3, E), tiles_b[0:E, :], tri[0:E, 0:E], start=True, stop=True).then_inc(starts_done, 1)
            pe.wait_ge(slots_ready, 1)

            pe.wait_ge(shared_in, 48)
            def shared(g):
                for hc in range(HC):
                    n = HC * g + hc
                    if n >= 2:
                        pe.wait_ge(hidden_done, n - 1)
                    s, at = hc // C, (hc % C) * P
                    for k, w in enumerate((swg_s, swu_s)):
                        for c in range(C):
                            mm = pe.matmul(bank(2 * (n % 2) + k), w[:, C * s + c, at:at + P],
                                           XT2[:, c, g * BANK:(g + 1) * BANK], start=(c == 0), stop=(c == C - 1))
                    mm.then_inc(up_done, 1)
                pe.wait_ge(hidden_done, HC * (g + 1))
                for t in range(4 * g, 4 * g + 4):
                    if t >= 2:
                        pe.wait_ge(shared_added, t - 1)
                    for hc in range(HC):
                        mm = pe.matmul(bank(4 + t % 2), hidden[:, hc, (t % 4) * P:(t % 4 + 1) * P], swd_s[:, hc, :],
                                       start=(hc == 0), stop=(hc == HC - 1))
                    mm.then_inc(down_done, 1)

            for g in range(EARLY):
                if g == EARLY - 1:
                    pe.wait_ge(table_float, 1)
                    pe.transpose(bank(6, PAIRS), tmp[:, 0:2, :].rearrange("p a b -> p (a b)")[0:PAIRS, :],
                                 ident[0:PAIRS, 0:PAIRS]).then_inc(table_turned, 1)
                shared(g)

            def turn_slots(n, k, i):
                j = k % JP
                pe.wait_ge(xg_in[j], 16 * (i + k // JP + 1))
                wait(pe, xgt_ready, n - 1)
                for c in range(C):
                    mm = pe.transpose(PS[:, (k % 2) * BANK + c * P:(k % 2) * BANK + (c + 1) * P],
                                      xg[:, j, c:D:C], ident[:, :])
                mm.then_inc(xg_turned, 1)

            def expert_up(n, j, i):
                for l in range(2):
                    pe.wait_ge(lane_up_in[2 * j + l], 32 * (i + 1))
                pe.wait_ge(xgt_ready, n + 1)
                wait(pe, e_hidden, n - 1)
                for c in range(C):
                    for l in range(2):
                        at = (2 + j % 2) * BANK
                        mm = pe.matmul(PS[l * SUB:(l + 1) * SUB, at:at + 2 * F],
                                       xgt[:, j % 2, c * P + l * SUB:c * P + (l + 1) * SUB],
                                       lane_w[2 * j + l][:, 0:2, c * F:(c + 1) * F], start=(c == 0), stop=(c == C - 1))
                mm.then_inc(e_up, 1)

            def turn_hidden(n, j):
                pe.wait_ge(e_hidden, n + 1)
                wait(pe, e_turned, n - 1)
                pe.transpose(bank(6 + j % 2, P), ht[:, j % 2, :], ident[:, :]).then_inc(e_turn, 1)

            def expert_down(n, j, i):
                for l in range(2):
                    pe.wait_ge(lane_down_in[2 * j + l], 16 * (i + 1))
                pe.wait_ge(e_turned, n + 1)
                wait(pe, yb_ready, n - 1)
                for l in range(2):
                    mm = pe.matmul(PS[l * SUB:(l + 1) * SUB, (4 + j % 2) * BANK:(5 + j % 2) * BANK],
                                   hg[:, j % 2, l * SUB:(l + 1) * SUB], lane_w[2 * j + l][:, 2, :],
                                   start=True, stop=True)
                mm.then_inc(e_down, 1)

            def expert_pairs(i, first, last):
                for j in range(JP):
                    n = JP * i + j
                    if not (last and j == JP - 1):
                        turn_slots(n + 1, j + 1, i)
                    expert_up(n, j, i)
                    if not (first and j < 1):
                        turn_hidden(n - 1, (j - 1) % JP)
                    if not (first and j < 2):
                        expert_down(n - 2, (j - 2) % JP, i if j >= 2 else i - 1)

            pe.wait_ge(table_ready, 1)
            turn_slots(0, 0, 0)
            expert_pairs(0, True, False)
            with pe.Fori(1, LANE_TILES - 1) as i:
                expert_pairs(i, False, False)
            expert_pairs(LANE_TILES - 1, False, True)
            turn_hidden(PAIRS - 1, JP - 1)
            expert_down(PAIRS - 2, JP - 2, LANE_TILES - 1)
            expert_down(PAIRS - 1, JP - 1, LANE_TILES - 1)

            pe.wait_ge(yb_ready, PAIRS)
            for g in range(EARLY, 4):
                shared(g)

        @block.vector
        def _(dve):
            def normalise_group(g):
                dve.wait_ge(x_in[g], 16)
                for t in range(4 * g, 4 * g + 4):
                    last = dve.bn_stats(stats[:, t, :], X[:, t, :])
                last.then_inc(ln_stats, 1)
                dve.wait_ge(ln_stats, g + 1)
                for t in range(4 * g, 4 * g + 4):
                    last = dve.bn_aggr(mv[:, t, :], stats[:, t, :])
                last.then_inc(ln_aggr, 1)
                dve.wait_ge(ln_std, g + 1)
                dve.reciprocal(rstd[:, 4 * g:4 * g + 4], std[:, 4 * g:4 * g + 4]).then_inc(ln_rstd, 1)
                dve.wait_ge(ln_rstd, g + 1)
                for t in range(4 * g, 4 * g + 4):
                    dve.tensor_scalar(XN[:, t, :], X[:, t, :], mv[:, t, 0:1], rstd[:, t:t + 1],
                                      ALU.subtract, ALU.mult).then_inc(xn_ready, 1)

            normalise_group(0)
            qk = 0
            for j, (kind, a) in enumerate(jobs):
                if kind == "T" and a % 4 == 0 and a // 4 + 1 < 4:
                    normalise_group(a // 4 + 1)
                if kind == "T" and a % 2 == 0:
                    dve.wait_ge(prep_done, j + 1)
                    dve.tensor_copy(XT[:, :, a * P:(a + 1) * P], bank(j % 8).rearrange("p (c t) -> p c t", c=C))\
                       .then_inc(xt_ready[0], 1)
                if kind == "QK":
                    dve.wait_ge(part_hi, qk + 1)
                    dve.tensor_tensor(rest[:, :], bank(j % 8), stage[:, qk % 2, 0, :], ALU.subtract)\
                       .then_inc(part_rest, 1)
                    dve.wait_ge(part_rest, qk + 1)
                    dve.tensor_copy(stage[:, qk % 2, 1, :], rest[:, :]).then_inc(part_mid, 1)
                    dve.wait_ge(part_mid, qk + 1)
                    dve.tensor_tensor(stage[:, qk % 2, 2, :], rest[:, :], stage[:, qk % 2, 1, :], ALU.subtract)\
                       .then_inc(part_low, 1)
                    dve.wait_ge(part_low, qk + 1)
                    qk += 1
                if kind == "V":
                    dve.wait_ge(prep_done, j + 1)
                    dve.tensor_copy(v_all[:, 4 * a:4 * a + 4, :, :],
                                    bank(j % 8).rearrange("p (t k d) -> p t k d", t=4, k=KVH)).then_inc(v_done, 1)

            def reduce_piece(b, k, index, parity):
                r = k // len(PIECES)
                qt, lo, n = PIECES[k % len(PIECES)]
                src = bank(4 + parity % 2, n)
                if lo + n == (qt + 1) * P:
                    wait_alone(dve, side_done, index + 1, dve_passed)
                    dve.tensor_tensor_reduce(out=junk[:, parity % 2, 0:n], in0=src, in1=causal[:, BANK - n:], scale=1.0,
                                             scalar=-3e38, op0=ALU.add, op1=ALU.max,
                                             accum_out=maxes[b][:, r, qt:qt + 1]).then_inc(side_read, 1)
                else:
                    dve.wait_ge(side_done, index + 1)
                    dve.reduce_max(max_low[:, r, qt - QT // 2:qt - QT // 2 + 1], src, AXX).then_inc(side_read, 1)

            def turn_rows(g, index, parity):
                dve.wait_ge(side_done, index + 1)
                src = bank(4 + parity % 2, P)[0:REP * QT, :]
                dve.tensor_scalar(max_rows[:, 0, :], src, -1.0, None, ALU.mult).then_inc(max_hi, 1)
                dve.wait_ge(max_hi, g + 1)
                dve.scalar_tensor_tensor(out=max_rows[:, 1, :], in0=src, scalar=-1.0, in1=max_rows[:, 0, :],
                                         op0=ALU.mult, op1=ALU.subtract).then_inc(side_read, 1)
                dve.wait_ge(side_read, index + 1)
                dve.sem_inc(rows_ready, 1)

            def side(index, parity, group, k):
                i, b = group
                if k is None:
                    turn_rows(BATCH * i + b, index, parity)
                else:
                    reduce_piece(b, k, index, parity)
                if k == SIDE - 2:
                    dve.wait_ge(side_read, index + 1)
                    dve.tensor_tensor(maxes[b][:, :, QT // 2:], maxes[b][:, :, QT // 2:], max_low[:, :, :],
                                      ALU.max).then_inc(max_ready, 1)

            def normalise(i, b, half, stage):
                g = BATCH * i + b
                n = 2 * g + half
                k = HALF // 32
                t = turned[:, :].rearrange("p (k f) -> p k f", f=32)
                if stage == 0:
                    dve.wait_ge(pv_done, NS * g + (NS if half else NS0))
                    wait(dve, z_done, n)
                    dve.transpose(turned[:, :], bank(6 + half)).then_inc(turn_done, 1)
                if stage == 1:
                    dve.wait_ge(turn_done, n + 1)
                    dve.reciprocal(recip[:, :], t[:, :, HD]).then_inc(recip_done, 1)
                if stage == 2:
                    dve.wait_ge(recip_done, n + 1)
                    dst = Z[:, b, half * k:(half + 1) * k, bass.ds(i, 1), :].rearrange("p k o e -> p k (o e)")
                    dve.tensor_tensor(dst, t[:, :, 0:HD], recip[:, :].unsqueeze(2).to_broadcast([P, k, HD]),
                                      ALU.mult).then_inc(z_done, 1)

            def group(i, b, last):
                for s in range(NS):
                    items = side_items(i, b, last, s)
                    for k in range(max(2, len(items))):
                        if k < len(items):
                            side(*items[k])
                        for first, half in ((2, 1), (NS0 + 3, 0)):
                            at = 2 * (s - first) + k
                            if k < 2 and at in (0, 1, 2) and not (half and isinstance(i, int) and i == 0 and b == 0):
                                if half:
                                    normalise(i - 1 + b, 1 - b, half, at)
                                else:
                                    normalise(i, b, half, at)

            dve.wait_ge(causal_set, 1)
            for item in FIRST_ITEMS:
                side(*item)
            for b in range(BATCH):
                group(0, b, False)
            with dve.Fori(1, KVH - 1) as i:
                for b in range(BATCH):
                    group(i, b, False)
            for b in range(BATCH):
                group(KVH - 1, b, True)
            for k in range(3):
                normalise(KVH - 1, 1, 1, k)
            dve.wait_ge(z_done, 4 * KVH)
            for b in range(BATCH):
                for c in range(C):
                    dve.transpose(YT[:, c, b * SEQ:(b + 1) * SEQ],
                                  Z[:, b, :, 2 * c:2 * c + 2, :].rearrange("p k h e -> p k (h e)")).then_inc(yt_done, 1)

            dve.wait_ge(yt_done, 2 * C)
            for g in range(4):
                ts = range(4 * g, 4 * g + 4)
                for t in ts:
                    dve.wait_ge(wo_done, t + 1)
                    dve.tensor_tensor(X[:, t, :], X[:, t, :], bank(t % 4), ALU.add).then_inc(x1_done, 1)
                dve.wait_ge(x1_done, 4 * g + 4)
                for t in ts:
                    last = dve.bn_stats(stats[:, t, :], X[:, t, :])
                last.then_inc(ln2_stats, 1)
                dve.wait_ge(ln2_stats, g + 1)
                for t in ts:
                    last = dve.bn_aggr(mv[:, t, :], stats[:, t, :])
                last.then_inc(ln2_aggr, 1)
                dve.wait_ge(ln2_std, g + 1)
                dve.reciprocal(rstd[:, 4 * g:4 * g + 4], std[:, 4 * g:4 * g + 4]).then_inc(ln2_rstd, 1)
                dve.wait_ge(ln2_rstd, g + 1)
                if g:
                    dve.wait_ge(xn2_stored, 64 * g)
                    dve.wait_ge(turn2_done, 4 * g)
                for t in ts:
                    dve.tensor_scalar(xn2[:, t % 4, :], X[:, t, :], mv[:, t, 0:1], rstd[:, t:t + 1],
                                      ALU.subtract, ALU.mult).then_inc(xn2_ready, 1)

            steps = [0]

            def step(ins):
                steps[0] += 1
                ins.then_inc(route, 1)
                dve.wait_ge(route, steps[0])

            dve.wait_ge(logits_done, NT)
            dve.wait_ge(consts, 13)
            log = PS[:, 6 * BANK:8 * BANK].rearrange("p (t e) -> p t e", t=NT)
            all_te = [P, NT, E]
            step(dve.tensor_reduce(lmax[:, :], log, AXX, ALU.max))
            step(dve.tensor_tensor(tmp[:, :, :], log, lmax[:, :].unsqueeze(2).to_broadcast(all_te), ALU.subtract))
            step(dve.tensor_tensor(biased[:, :, :], log, bias_s[:, :].unsqueeze(1).to_broadcast(all_te), ALU.add))
            for t in range(NT):
                last = dve.max(top8[:, t, :], biased[:, t, :])
            step(last)
            for t in range(NT):
                last = dve.max_index(idx8[:, t, :], top8[:, t, :], biased[:, t, :])
            step(last)
            step(dve.tensor_copy(idxf[:, :, :], idx8[:, :, :]))
            dve.wait_ge(ex_ready, 1)
            for k in range(TOPK):
                step(dve.tensor_tensor(onehot[k][:, :, :], iota_e[:, :].unsqueeze(1).to_broadcast(all_te),
                                       idxf[:, :, k:k + 1].to_broadcast(all_te), ALU.is_equal))
                step(dve.tensor_tensor(tmp[:, :, :], onehot[k][:, :, :], ex[:, :, :], ALU.mult))
                step(dve.tensor_reduce(part_k[:, k, :], tmp[:, :, :], AXX, ALU.add))
                if k == 1:
                    step(dve.tensor_tensor(mask[:, :, :], onehot[0][:, :, :], onehot[1][:, :, :], ALU.add))
                if k > 1:
                    step(dve.tensor_tensor(mask[:, :, :], mask[:, :, :], onehot[k][:, :, :], ALU.add))
            step(dve.memset(cum[:, 0, :], 0.0))
            for t in range(1, NT):
                step(dve.tensor_tensor(cum[:, t, :], cum[:, t - 1, :], mask[:, t - 1, :], ALU.add))
            step(dve.tensor_tensor(total_b[:, :], cum[:, NT - 1, :], mask[:, NT - 1, :], ALU.add))
            dve.sem_inc(masks_ready, 1)
            step(dve.tensor_tensor(lmax[:, :], part_k[:, 0, :], part_k[:, 1, :], ALU.add))
            for k in range(2, TOPK):
                step(dve.tensor_tensor(lmax[:, :], lmax[:, :], part_k[:, k, :], ALU.add))
            step(dve.reciprocal(lmax[:, :], lmax[:, :]))
            step(dve.tensor_tensor(gates[:, :, :], part_k[:, :, :], lmax[:, :].unsqueeze(1).to_broadcast([P, TOPK, NT]),
                                   ALU.mult))
            dve.wait_ge(ranks_done, 1)
            step(dve.tensor_copy(counts[0:E, 0:1], bank(2, 1)[0:E, :]))
            step(dve.tensor_scalar(idxf[0:E, 0:4, :].rearrange("p a b -> p (a b)"), iota_c[0:E, :], counts[0:E, 0:1], None,
                                   ALU.is_lt))
            step(dve.tensor_reduce(counts[0:E, 1:2], idxf[0:E, 0:4, :].rearrange("p a b -> p (a b)"), AXX, ALU.add))
            step(dve.tensor_scalar(tiles_b[0:E, :], ones_b[0:E, :], counts[0:E, 1:2], None, ALU.mult))
            dve.sem_inc(tiles_ready, 1)
            dve.wait_ge(starts_done, 1)
            step(dve.tensor_copy(start_s[:, :], bank(3, E)))
            i24, all_se = slice(0, LANE_TILES), [LANE_TILES, 2 * LANES, E]
            step(dve.tensor_tensor(tmp[i24, :, :], start_s[i24, :].unsqueeze(1).to_broadcast(all_se),
                                   tile_no[i24, :].unsqueeze(2).to_broadcast(all_se), ALU.is_le))
            step(dve.tensor_reduce(found[i24, :], tmp[i24, :, :], AXX, ALU.add))
            step(dve.tensor_tensor(found[i24, LANES:], found[i24, 0:LANES], found[i24, LANES:], ALU.not_equal))
            step(dve.tensor_scalar(found[i24, 0:LANES], found[i24, 0:LANES], -1.0, None, ALU.add))
            step(dve.scalar_tensor_tensor(out=code[i24, :], in0=found[i24, LANES:], scalar=float(E),
                                          in1=found[i24, 0:LANES], op0=ALU.mult, op1=ALU.add))
            dve.sem_inc(experts_ready, 1)
            step(dve.tensor_scalar(start_s[:, :], start_s[:, :], float(SUB), None, ALU.mult))
            step(dve.tensor_tensor(pos[:, :, :], PS[:, 0:2 * BANK].rearrange("p (t e) -> p t e", t=NT),
                                   start_s[:, :].unsqueeze(1).to_broadcast(all_te), ALU.add))
            for k in range(TOPK):
                step(dve.tensor_tensor(tmp[:, :, :], onehot[k][:, :, :], pos[:, :, :], ALU.mult))
                step(dve.tensor_reduce(part_k[:, k, :], tmp[:, :, :], AXX, ALU.add))
            step(dve.tensor_copy(slot_u[:, :, :], part_k[:, :, :]))
            dve.sem_inc(slots_ready, 2)

            def shared_hidden(n):
                dve.wait_ge(silu_done, n + 1)
                dve.tensor_tensor(hidden[:, n % HC, :], silu_s[:, n % 2, :], bank(2 * (n % 2) + 1), ALU.mult)\
                   .then_inc(hidden_done, 1)

            def shared_add(t):
                dve.wait_ge(down_done, t + 1)
                dve.tensor_tensor(X[:, t, :], X[:, t, :], bank(4 + t % 2), ALU.add).then_inc(shared_added, 1)

            for g in range(EARLY):
                if g:
                    dve.wait_ge(down_done, 4 * g)
                if g == EARLY - 1:
                    dve.wait_ge(table_in, 16 * LANES)
                    flat_tmp = tmp[:, 0:2, :].rearrange("p a b -> p (a b)")
                    dve.tensor_copy(flat_tmp[0:PAIRS, :], tab[0:PAIRS, :]).then_inc(table_float, 1)
                    dve.wait_ge(table_turned, 1)
                    dve.tensor_copy(tab_t[:, :], bank(6, PAIRS)).then_inc(table_ready, 1)
                for n in range(HC * g, HC * (g + 1)):
                    shared_hidden(n)
                for t in range(4 * g, 4 * g + 4):
                    shared_add(t)

            def expert_hidden(n, j):
                dve.wait_ge(e_silu, n + 1)
                wait(dve, e_turn, n - 1)
                dve.tensor_tensor(ht[:, j % 2, :], sg[:, j % 2, :], PS[:, (2 + j % 2) * BANK + F:(2 + j % 2) * BANK + 2 * F],
                                  ALU.mult).then_inc(e_hidden, 1)

            def hidden_turned(n, j):
                dve.wait_ge(e_turn, n + 1)
                wait(dve, e_down, n - 1)
                dve.tensor_copy(hg[:, j % 2, :], bank(6 + j % 2, P)).then_inc(e_turned, 1)

            def expert_y(n, j, count):
                dve.wait_ge(e_down, n + 1)
                wait(dve, yb_stored[j % 2], 32 * count)
                dve.tensor_copy(yb[:, j % 2, :], bank(4 + j % 2)).then_inc(yb_ready, 1)

            def expert_pairs(i, first, last):
                for j in range(JP):
                    n = JP * i + j
                    expert_hidden(n, j)
                    if not (first and j < 1):
                        hidden_turned(n - 1, (j - 1) % JP)
                    if not (first and j < 2):
                        expert_y(n - 2, (j - 2) % JP, 2 * i + (j - 2) // 2)

            expert_pairs(0, True, False)
            with dve.Fori(1, LANE_TILES - 1) as i:
                expert_pairs(i, False, False)
            expert_pairs(LANE_TILES - 1, False, True)
            hidden_turned(PAIRS - 1, JP - 1)
            expert_y(PAIRS - 2, JP - 2, PAIRS // 2 - 1)
            expert_y(PAIRS - 1, JP - 1, PAIRS // 2 - 1)

            def mix(t):
                dve.wait_ge(yk_in[t % YK], 16 * TOPK * (t // YK + 1))
                for k in range(TOPK):
                    if k:
                        dve.wait_ge(mixed, TOPK * t + k)
                    else:
                        dve.wait_ge(shared_added, t + 1)
                    dve.scalar_tensor_tensor(out=X[:, t, :], in0=yk[:, t % YK, k, :], scalar=gates[:, k, t:t + 1],
                                             in1=X[:, t, :], op0=ALU.mult, op1=ALU.add).then_inc(mixed, 1)

            mixed_tiles = 0
            for n in range(HC * EARLY, HC * 4):
                shared_hidden(n)
                while mixed_tiles < (n - HC * EARLY + 1) * 4 * EARLY // HC:
                    mix(mixed_tiles)
                    mixed_tiles += 1
            for t in range(4 * EARLY, NT):
                shared_add(t)
                mix(t)


_INS = ['L0_attn_x', 'L0_attn_wq', 'L0_attn_wk', 'L0_attn_wv', 'L0_attn_wo', 'L0_ffn_router_w', 'L0_ffn_router_bias',
        'L0_ffn_wg', 'L0_ffn_wu', 'L0_ffn_wd', 'L0_ffn_swg', 'L0_ffn_swu', 'L0_ffn_swd']
_OUTS = [((BATCH, SEQ, D), 'float32')]


def kernel(**inputs):
    import numpy as _np
    import concourse.bacc as _bacc
    from concourse import mybir as _mybir
    from concourse.bass_utils import run_bass_kernel_spmd as _run

    nc = _bacc.Bacc("TRN2", target_bir_lowering=False, num_devices=1)
    arrays, args = {}, []
    for name in _INS:
        a = _np.ascontiguousarray(inputs[name])
        arrays[f"in_{name}_dram"] = a
        args.append(nc.dram_tensor(f"in_{name}_dram", a.shape, _mybir.dt.from_np(a.dtype), kind="ExternalInput").ap())
    for i, (shape, dtype) in enumerate(_OUTS):
        dt = _mybir.dt.from_np(_np.dtype(dtype))
        args.append(nc.dram_tensor(f"out_{i}_dram", shape, dt, kind="ExternalOutput").ap())
    build_block(nc, *args)
    r = _run(nc, [arrays], core_ids=[0])
    return r.results[0]["out_0_dram"]
```

```python
import concourse.bass as bass
from concourse import mybir
from contextlib import ExitStack

FP32 = mybir.dt.float32
BF16 = mybir.dt.bfloat16
F16 = mybir.dt.float16
U32 = mybir.dt.uint32
ACT = mybir.ActivationFunctionType
ALU = mybir.AluOpType
AXX = mybir.AxisListType.X

P = 128
BATCH, SEQ, D = 2, 1024, 512
NTOK = BATCH * SEQ
NT = NTOK // P
C = D // P
HEADS, KVH, HD = 32, 8, 16
REP = HEADS // KVH
QT = SEQ // P
BANK = 512
E, F, TOPK = 64, 128, 4
HID = 1024
HC = HID // P
SUB = P // 2
LANES = 8
LANE_TILES = -(-((TOPK * NTOK - E) // SUB + E) // LANES)
SLOTS = LANES * LANE_TILES * SUB
JP = LANES // 2
PAIRS = JP * LANE_TILES
EARLY = 2
TABLE_AT = 4 * EARLY - 3
RANKS_AT = 5
STARTS_AT = 6
YK = 3
EPS = 1e-5
NEG = -1e30
X_SCALE, W_SCALE = 16.0, 64.0

Q_PART = [0, 0, 1, 1, 0, 2]
K_PART = [0, 1, 0, 1, 2, 0]
STACK = len(Q_PART) * HD
KROWS = STACK + 2

HALF = SEQ // 2
WIN = SEQ // REP


def steps_of_half(half):
    full, odd = [], []
    for kt in range((half + 1) * HALF // P):
        q = max(kt * P, half * HALF)
        if q % WIN:
            odd.append((kt, q, P))
            q += P
        full += [[(kt, a, WIN, 0)] for a in range(q, (half + 1) * HALF, WIN)]
    pairs = [[(*odd[n], 0), (*odd[n + 1], REP * P)] for n in range(0, len(odd), 2)]
    return full + pairs


STEPS = steps_of_half(0) + steps_of_half(1)
NS = len(STEPS)
NS0 = len(steps_of_half(0))
PIECES = [(qt, lo, min(512, (qt + 1) * P - lo)) for qt in range(QT) for lo in range(0, (qt + 1) * P, 512)]
SIDE = REP * len(PIECES) + 1
LATE = 4
AHEAD = 16
MASKS = sum(x[0][1] == x[0][0] * P for x in STEPS)


TURN_1 = 1
TURN_0 = NS0 + 2
SIDE_BANKS = (4, 5)
SUM_BANKS = (6, 7)


def banks_of_slots():
    at, used = [], {}
    for turn in range(4):
        for s in range(NS):
            for k in range(AHEAD + s * SIDE // NS, AHEAD + (s + 1) * SIDE // NS):
                free = SIDE_BANKS
                if TURN_1 < s < NS0:
                    free += SUM_BANKS[1:]
                if TURN_0 < s:
                    free += SUM_BANKS[:1]
                n = SIDE * turn + k
                b = min(free, key=lambda x: used.get(x, -1))
                at.append((b, n - used.get(b, n - 1)))
                used[b] = n
    assert at[-2 * SIDE:-SIDE] == at[-SIDE:]
    return at[-SIDE:]


SLOTS_AT = banks_of_slots()
LAST_IN = [max(AHEAD + n for n in range(SIDE) if SLOTS_AT[n][0] == b) for b in SUM_BANKS]


def side_items(i, b, last, s):
    found = []
    for k in range(AHEAD + s * SIDE // NS, AHEAD + (s + 1) * SIDE // NS):
        bank, before = SLOTS_AT[k - AHEAD]
        if isinstance(i, int) and i == 0 and b == 0 and before > k - AHEAD:
            before = 1
        place = SIDE * (BATCH * i + b + 1) + k - 1
        if (k < SIDE and not (last and b == 1)) or (k >= SIDE and not last):
            g, n = ((i + b, 1 - b), (i + 1, b))[k // SIDE], k % SIDE
            if n == LATE:
                g, n = ((i, b), (i + b, 1 - b))[k // SIDE], None
            else:
                n -= n > LATE
            found.append((place, bank, before, g, n))
        elif k == SIDE + LATE and b == 0:
            found.append((SIDE * BATCH * KVH - 1, bank, 1, (i, 1), None))
    return found


def first_item(k):
    n = k - (SIDE - 1)
    if n < 0:
        return k, SIDE_BANKS[k % 2], 2, (0, 0), k
    return k, SIDE_BANKS[k % 2], 2, (0, 0 if n == LATE else 1), None if n == LATE else n - (n > LATE)


FIRST_ITEMS = [first_item(k) for k in range(SIDE - 1 + AHEAD)]


def wait(eng, sem, value):
    if not (isinstance(value, int) and value <= 0):
        eng.wait_ge(sem, value)


def wait_alone(eng, sem, value, passed):
    eng.wait_ge(sem, value)
    eng.sem_inc(passed, 1)


def build_block(nc, x, wq, wk, wv, wo, router_w, router_bias, wg, wu, wd, swg, swu, swd, out):
    ctx = ExitStack()
    with ctx:
        def sb(name, shape, dt=FP32):
            return ctx.enter_context(nc.sbuf_tensor(name, shape, dt))

        def sem(name):
            return ctx.enter_context(nc.semaphore(name))

        def carve(arena, at, shape, dt=FP32):
            n = 1
            for d in shape[1:]:
                n *= d
            words = n * (2 if dt in (BF16, F16) else 4) // 4
            v = arena[0:shape[0], at:at + words]
            if dt != FP32:
                v = v.bitcast(dt)
            if len(shape) == 3:
                v = v.rearrange("p (a b) -> p a b", a=shape[1])
            if len(shape) == 4:
                v = v.rearrange("p (a b c) -> p a b c", a=shape[1], b=shape[2])
            return v, at + words

        def carve_all(arena, at, *wanted):
            views = []
            for shape, dt in wanted:
                v, at = carve(arena, at, shape, dt)
                views.append(v)
            return views

        qk_parts = nc.dram_tensor("qk_parts", [3, D + KVH * HD, NTOK], BF16)
        xn2_rows = nc.dram_tensor("xn2_rows", [NTOK, D], FP32)
        slot_tokens = nc.dram_tensor("slot_tokens", [SLOTS, 1], U32)
        slot_y = nc.dram_tensor("slot_y", [SLOTS, D], FP32)

        X = sb("X", [P, NT, D])
        XN = sb("XN", [P, NT, D])
        XT = sb("XT", [P, C, NTOK])
        att = sb("att", [P, 14336])
        w_att = sb("w_att", [P, 5120])
        ring = sb("ring", [P, 4 * 3 * C * F])
        small = sb("small", [P, 1536])
        ident = sb("ident", [P, P])
        eps_s = sb("eps_s", [P, 1])
        stats = sb("stats", [P, NT, 6])
        mv = sb("mv", [P, NT, 2])
        std = sb("std", [P, NT])
        rstd = sb("rstd", [P, NT])
        v_head = [sb(f"v_head{b}", [P, QT, 2 * HD]) for b in range(BATCH)]
        maxes = [sb(f"maxes{b}", [P, REP, QT]) for b in range(BATCH)]
        max_low = sb("max_low", [P, REP, QT // 2])
        max_rows = sb("max_rows", [REP * QT, 2, P], BF16)
        recip = sb("recip", [P, HALF // 32])
        router_s = sb("router_s", [P, C, E])
        bias_s = sb("bias_s", [P, E])

        wq_s, wk_s, wv_s, wo_s = carve_all(w_att, 0, ([P, C, D], FP32), ([P, C, KVH * HD], FP32),
                                           ([P, C, KVH * HD], FP32), ([P, C, D], FP32))
        v_all = carve(ring, 0, [P, NT, KVH * HD])[0].rearrange("p t (k d) -> p t k d", k=KVH)
        probs, *stacks = carve_all(att, 0, ([P, 4, REP * WIN], FP32), *[([P, REP, SEQ], BF16)] * 4,
                                   *[([P, SEQ], BF16)] * 4)
        q_max, q_exp, k_max, k_exp = stacks[0:2], stacks[2:4], stacks[4:6], stacks[6:8]
        stage, rest = carve_all(att, 0, ([P, 2, 3 * BANK], BF16), ([P, BANK], FP32))
        stage = stage.rearrange("p n (a t) -> p n a t", a=3)
        turned, causal = carve_all(small, 0, ([P, HALF], FP32), ([P, BANK], FP32))
        junk, = carve_all(ring, 2048, ([P, 4, BANK], BF16))
        Z = XN[:, :, :].rearrange("p n d -> p (n d)").rearrange("p (b k h e) -> p b k h e", b=BATCH, h=KVH, e=HD)
        YT = XT

        flat_xn = XN[:, :, :].rearrange("p n d -> p (n d)")
        flat_xt = XT[:, :, :].rearrange("p c t -> p (c t)")
        x_hi, x_lo = carve_all(flat_xn, 0, *[([P, C, NTOK], F16)] * 2)
        w_stage, x_turned = carve_all(ring, 0, ([P, 2, C * D], FP32), ([P, 4, C * P], FP32))
        x_turned = x_turned.rearrange("p n (c t) -> p n c t", c=C)
        xn2, = carve_all(w_att, 0, ([P, 4, D], FP32))
        shared_w, swd_s, tmp, mask, cum = carve_all(
            att, 0, ([P, 4, 2 * C * D], F16), ([P, HC, D], FP32), ([P, NT, E], FP32),
            ([P, NT, E], BF16), ([P, NT, E], BF16))
        shared_w = shared_w.rearrange("p n (s d) -> p n s d", s=2 * C)
        hidden, biased, ex, *onehot = carve_all(
            flat_xt, 0, ([P, HC, BANK], FP32), ([P, NT, E], FP32), ([P, NT, E], FP32), *[([P, NT, E], BF16)] * TOPK)
        pos = biased
        row_e = carve(att, 13312, [1, LANES * LANE_TILES], U32)[0]
        silu_s, = carve_all(w_att, 4096, ([P, 2, BANK], FP32))
        up_s, = carve_all(w_att, 2048, ([P, 2, BANK], FP32))
        (tri, ones_b, iota_e, top8, idx8, idxf, part_k, gates, slot_u, tab, tab_t, lmax, counts, start_s, tile_no,
         total_b, tiles_b, iota_c, token_ids, found, code) = carve_all(
            small, 0, ([P, P], BF16), ([P, P], BF16), ([P, E], FP32), ([P, NT, 8], FP32), ([P, NT, 8], U32),
            ([P, NT, 8], FP32), ([P, TOPK, NT], FP32), ([P, TOPK, NT], FP32), ([P, TOPK, NT], U32),
            ([P, P], U32), ([P, PAIRS], U32), ([P, NT], FP32), ([P, 2], FP32), ([P, E], FP32),
            ([P, 2 * LANES], FP32), ([P, E], BF16), ([P, P], BF16), ([P, NTOK // SUB], FP32), ([P, NT], U32),
            ([P, 2 * LANES], FP32), ([P, LANES], U32))
        lane_w = [carve(ring, n * 3 * C * F, [P, 3, C * F])[0] for n in range(4)]
        lane_w += [carve(flat_xt, n * 3 * C * F, [P, 3, C * F])[0] for n in range(4)]
        xg, xgt, yb, sg, ht, hg = carve_all(w_att, 0, ([P, 4, D], FP32), ([P, 2, D], FP32), ([P, 2, D], FP32),
                                            ([P, 2, P], FP32), ([P, 2, P], FP32), ([P, 2, P], FP32))
        idx = sb("idx", [P, 4], U32)
        yk = carve(ring, 0, [P, YK, TOPK, D])[0]

        PS = ctx.enter_context(nc.psum_tensor("PS", [P, 8 * BANK], FP32))

        def bank(k, n=BANK):
            return PS[:, k * BANK:k * BANK + n]

        x_in = [sem(f"x_in{g}") for g in range(4)]
        w_in = sem("w_in")
        pool_passed = sem("pool_passed")
        dve_passed = sem("dve_passed")
        eps_set = sem("eps_set")
        ident_zero = sem("ident_zero")
        ident_set = sem("ident_set")
        causal_zero = sem("causal_zero")
        causal_set = sem("causal_set")
        v_ones = sem("v_ones")
        k_ones = sem("k_ones")
        ln_stats = sem("ln_stats")
        ln_aggr = sem("ln_aggr")
        ln_std = sem("ln_std")
        ln_rstd = sem("ln_rstd")
        xn_ready = sem("xn_ready")
        prep_done = sem("prep_done")
        xt_ready = [sem("xt_ready_dve"), sem("xt_ready_act")]
        part_hi = sem("part_hi")
        part_rest = sem("part_rest")
        part_mid = sem("part_mid")
        part_low = sem("part_low")
        parts_out = [sem("parts_out0"), sem("parts_out1")]
        v_done = sem("v_done")

        max_in = [sem("max_in0"), sem("max_in1")]
        exp_in = [sem("exp_in0"), sem("exp_in1")]
        v_in = [sem("v_in0"), sem("v_in1")]
        side_done = sem("side_done")
        side_read = sem("side_read")
        max_ready = sem("max_ready")
        max_hi = sem("max_hi")
        rows_ready = sem("rows_ready")
        rows_in = sem("rows_in")
        scores_done = sem("scores_done")
        exp_done = sem("exp_done")
        masked = sem("masked")
        pv_done = sem("pv_done")
        turn_done = sem("turn_done")
        recip_done = sem("recip_done")
        z_done = sem("z_done")
        yt_done = sem("yt_done")

        shared_in = sem("shared_in")
        x1_done = sem("x1_done")
        ln2_stats = sem("ln2_stats")
        ln2_aggr = sem("ln2_aggr")
        ln2_std = sem("ln2_std")
        ln2_rstd = sem("ln2_rstd")
        wo_done = sem("wo_done")
        xn2_ready = sem("xn2_ready")
        xn2_stored = sem("xn2_stored")
        turn2_done = sem("turn2_done")
        xt2_ready = sem("xt2_ready")
        x_hi_ready = sem("x_hi_ready")
        x_lo_ready = sem("x_lo_ready")
        w_hi_ready = sem("w_hi_ready")
        w_lo_ready = sem("w_lo_ready")
        stage_in = [sem("stage_in0"), sem("stage_in1")]
        logits_done = sem("logits_done")
        consts = sem("consts")
        route = sem("route")
        ex_ready = sem("ex_ready")
        masks_ready = sem("masks_ready")
        ranks_done = sem("ranks_done")
        tiles_ready = sem("tiles_ready")
        starts_done = sem("starts_done")
        slots_ready = sem("slots_ready")
        table_zero = sem("table_zero")
        table_set = sem("table_set")
        table_in = sem("table_in")
        table_float = sem("table_float")
        table_turned = sem("table_turned")
        table_ready = sem("table_ready")
        experts_ready = sem("experts_ready")
        experts_in = sem("experts_in")
        up_done = sem("up_done")
        silu_done = sem("silu_done")
        up_copied = sem("up_copied")
        hidden_done = sem("hidden_done")
        down_done = sem("down_done")
        shared_added = sem("shared_added")

        lane_up_in = [sem(f"lane_up_in{n}") for n in range(LANES)]
        lane_down_in = [sem(f"lane_down_in{n}") for n in range(LANES)]
        idx_set = sem("idx_set")
        xg_in = [sem(f"xg_in{j}") for j in range(4)]
        xg_turned = sem("xg_turned")
        xgt_ready = sem("xgt_ready")
        e_up = sem("e_up")
        e_silu = sem("e_silu")
        e_hidden = sem("e_hidden")
        e_turn = sem("e_turn")
        e_turned = sem("e_turned")
        e_down = sem("e_down")
        yb_ready = sem("yb_ready")
        yb_stored = [sem("yb_stored0"), sem("yb_stored1")]
        yk_in = [sem(f"yk_in{n}") for n in range(YK)]
        mixed = sem("mixed")
        stored = sem("stored")

        x_view = x.rearrange("b (n p) d -> p (b n) d", p=P)
        out_view = out.rearrange("b (n p) d -> p (b n) d", p=P)

        jobs = [("T", t) for t in range(4)]
        for g in range(4):
            jobs += [("T", t) for t in range(4 * g + 4, min(4 * g + 8, NT))]
            jobs += [("QK", (m, g)) for m in (0, C, 1, 2, 3)] + [("V", g)]
        QK_JOBS = (C + 1) * 4
        PARTS_OUT = [C + 3, 3 * (C + 1) + 2]
        STACK_LOADS = 3
        MIX, INNER = jobs.index(("QK", (0, 2))), 4
        inner, items = [], iter(FIRST_ITEMS[:SIDE - 1])
        for j, (kind, a) in enumerate(jobs):
            inner.append([next(items) for _ in range(INNER)] if j >= MIX and kind != "T" else [])
        inner.append([])
        rest_items = FIRST_ITEMS[sum(len(n) for n in inner):]
        banks, bank_user, used = [], [], {}
        for j in range(len(jobs)):
            free = [k for k in range(8) if j < MIX - 3 or k not in SIDE_BANKS]
            banks.append(min(free, key=lambda k: used.get(k, -1)))
            bank_user.append(used.get(banks[j]))
            used[banks[j]] = j
        side_user = [used[k] for k in SIDE_BANKS]

        block = ctx.enter_context(nc.Block())

        @block.sync
        def _(sp):
            for g in range(4):
                sp.dma_start(X[:, 4 * g:4 * g + 4, :], x_view[:, 4 * g:4 * g + 4, :]).then_inc(x_in[g], 16)
            def load_stack(q, k, i, b, done, parts=range(len(Q_PART))):
                at = slice(b * SEQ, (b + 1) * SEQ)
                for j in parts:
                    sp.dma_start(q[b][j * HD:(j + 1) * HD, :, :],
                                 qk_parts[Q_PART[j], bass.ds(i * (REP * HD), REP * HD), at]
                                 .rearrange("(r d) t -> d r t", r=REP)).then_inc(done[b], 16)
                    sp.dma_start(k[b][j * HD:(j + 1) * HD, :],
                                 qk_parts[K_PART[j], bass.ds(i * HD + D, HD), at]).then_inc(done[b], 16)

            for n, (m, g) in enumerate([a for k, a in jobs if k == "QK"]):
                sp.wait_ge(part_low, n + 1)
                sp.dma_start(qk_parts[:, m * P:(m + 1) * P, g * BANK:(g + 1) * BANK].rearrange("a p t -> p a t"),
                             stage[:, n % 2, :, :]).then_inc(parts_out[n % 2], 16)
                for b, first in enumerate(PARTS_OUT):
                    if n == first:
                        for k in range(2):
                            sp.wait_ge(parts_out[k], 16 * ((first + 1 - k) // 2))
                    some = len(Q_PART) // STACK_LOADS
                    for q, k, done in ((q_max, k_max, max_in), (q_exp, k_exp, exp_in)):
                        if first <= n < first + STACK_LOADS:
                            load_stack(q, k, 0, b, done, range(some * (n - first), some * (n - first + 1)))
                        first += STACK_LOADS
            for s in parts_out:
                sp.wait_ge(s, 16 * QK_JOBS // 2)

            def group(i, b, last):
                g = BATCH * i + b
                if not last:
                    sp.wait_ge(side_done, SIDE * g + SIDE - 1)
                    load_stack(q_max, k_max, i + 1, b, max_in)
                if not (last and b == BATCH - 1):
                    sp.wait_ge(rows_ready, g + 2)
                    for h in range(2):
                        sp.dma_start(q_exp[1 - b][STACK + h:STACK + h + 1, :, :], max_rows[:, h, :])\
                          .then_inc(rows_in, 16)
                if not last:
                    sp.wait_ge(scores_done, NS * (g + 1))
                    load_stack(q_exp, k_exp, i + 1, b, exp_in)

            sp.wait_ge(rows_ready, 1)
            for h in range(2):
                sp.dma_start(q_exp[0][STACK + h:STACK + h + 1, :, :], max_rows[:, h, :]).then_inc(rows_in, 16)
            load_stack(q_exp, k_exp, 0, 1, exp_in)
            for b in range(BATCH):
                group(0, b, False)
            with sp.Fori(1, KVH - 1) as i:
                for b in range(BATCH):
                    group(i, b, False)
            for b in range(BATCH):
                group(KVH - 1, b, True)
            sp.wait_ge(z_done, 4 * KVH)
            def load_stage(k):
                if k >= 2:
                    sp.wait_ge(w_lo_ready, k - 1)
                sp.dma_start(w_stage[:, k % 2, :].rearrange("p (c n) -> p c n", c=C),
                             (swg, swu)[k // 2][k % 2].rearrange("(c p) n -> p c n", p=P)).then_inc(stage_in[k % 2], 16)

            load_stage(0)
            load_stage(1)
            sp.dma_start(swd_s.rearrange("p (s c) n -> p s c n", s=2), swd.rearrange("s (c p) n -> p s c n", p=P))\
              .then_inc(shared_in, 16)
            for t in range(NT):
                sp.wait_ge(xn2_ready, t + 1)
                sp.dma_start(xn2_rows[t * P:(t + 1) * P, :], xn2[:, t % 4, :]).then_inc(xn2_stored, 16)
                if t in (3, 7):
                    load_stage(2 + t // 4)
            sp.wait_ge(experts_ready, 1)
            sp.dma_start(row_e[0:1, :], code[0:LANE_TILES, :]).then_inc(experts_in, 16)
            sp.wait_ge(table_set, 16 * TOPK * NT)
            for n in range(LANES):
                j, l = n // 2, n % 2
                sp.dma_start(tab[j * LANE_TILES:(j + 1) * LANE_TILES, l * SUB:(l + 1) * SUB],
                             slot_tokens[n * LANE_TILES * SUB:(n + 1) * LANE_TILES * SUB, :]
                             .rearrange("(i q) o -> i (q o)", q=SUB)).then_inc(table_in, 16)

            def load_up(i, j):
                codes = []
                for n in (2 * j, 2 * j + 1):
                    code = sp.value_load(row_e[0:1, bass.ds(i * LANES + n, 1)], min_val=0, max_val=2 * E - 1)
                    e, new = sp.snap(code % E, min_val=0, max_val=E - 1), sp.snap(code // E, min_val=0, max_val=1)
                    codes.append((e, new))
                    wait(sp, e_up, JP * (i - 1) + j + 1)
                    for k, w in enumerate((wg, wu)):
                        sp.dma_start(lane_w[n][:, k, :],
                                     w[bass.ds(e, 1), :, :].rearrange("o (p c) f -> p (o c f)", c=C),
                                     cond=new).then_inc(lane_up_in[n], 16)
                return codes

            def load_down(i, j, codes):
                for n, (e, new) in zip((2 * j, 2 * j + 1), codes):
                    wait(sp, e_down, JP * (i - 1) + j + 1)
                    sp.dma_start(lane_w[n][:, 2, :], wd[bass.ds(e, 1), :, :].rearrange("o f d -> f (o d)"),
                                 cond=new).then_inc(lane_down_in[n], 16)

            def load_pairs(i, first):
                codes = []
                for j in range(JP):
                    if first and j == 2:
                        sp.wait_ge(down_done, 4 * EARLY)
                    codes.append(load_up(i, j))
                    if j:
                        load_down(i, j - 1, codes[j - 1])
                load_down(i, JP - 1, codes[JP - 1])

            sp.wait_ge(experts_in, 16)
            load_pairs(0, True)
            with sp.Fori(1, LANE_TILES) as i:
                load_pairs(i, False)
            for t in range(NT):
                sp.wait_ge(mixed, TOPK * (t + 1))
                if t >= NT - 4:
                    sp.wait_ge(shared_added, t + 1)
                sp.dma_start(out_view[:, t, :], X[:, t, :]).then_inc(stored, 16)
            sp.wait_ge(stored, 16 * NT)

        @block.gpsimd
        def _(pool):
            pool.memset(eps_s[:, :], EPS).then_inc(eps_set, 1)
            pool.memset(ident[:, :], 0.0).then_inc(ident_zero, 1)
            pool.wait_ge(ident_zero, 1)
            pool.affine_select(out=ident[:, :], in_=ident[:, :], compare_op=ALU.not_equal, fill=1.0, base=0,
                               pattern=[[-1, P]], channel_multiplier=1).then_inc(ident_set, 1)
            for b in range(BATCH):
                pool.memset(v_head[b][:, :, :], 1.0).then_inc(v_ones, 1)
            pool.memset(causal[:, :], 0.0).then_inc(causal_zero, 1)
            pool.wait_ge(causal_zero, 1)
            pool.affine_select(out=causal[:, BANK - P:], in_=causal[:, BANK - P:], compare_op=ALU.is_ge, fill=NEG,
                               base=0, pattern=[[-1, P]], channel_multiplier=1).then_inc(causal_set, 1)
            pool.wait_ge(causal_set, 1)
            for b in range(BATCH):
                pool.memset(k_exp[b][STACK:KROWS, :], 1.0).then_inc(k_ones, 1)
                pool.wait_ge(k_ones, b + 1)

            def load_v(i, b):
                pool.tensor_copy(v_head[b][:, :, 0:HD], v_all[:, b * QT:(b + 1) * QT, bass.ds(i, 1), :]
                                 .rearrange("p t o e -> p t (o e)")).then_inc(v_in[b], 1)

            def divide(i, b, half):
                n = 2 * (BATCH * i + b) + half
                k = HALF // 32
                pool.wait_ge(recip_done, n + 1)
                pool.tensor_tensor(Z[:, b, half * k:(half + 1) * k, bass.ds(i, 1), :].rearrange("p k o e -> p k (o e)"),
                                   turned[:, :].rearrange("p (k f) -> p k f", f=32)[:, :, 0:HD],
                                   recip[:, :].unsqueeze(2).to_broadcast([P, k, HD]), ALU.mult).then_inc(z_done, 1)

            def group(i, b, last):
                g = BATCH * i + b
                for s, segments in enumerate(STEPS):
                    if s == TURN_1 + 1 and not (isinstance(i, int) and i == 0 and b == 0):
                        divide(i - 1 + b, 1 - b, 1)
                    if s == TURN_0 + 1:
                        divide(i, b, 0)
                    if s == 3 and not (last and b == 1):
                        wait(pool, pv_done, NS * g)
                        load_v(i + b, 1 - b)
                    if segments[0][1] != segments[0][0] * P:
                        continue
                    wait_alone(pool, exp_done, NS * g + s + 1, pool_passed)
                    n = len(segments) * REP
                    d = probs[:, (NS * b + s) % 4, :].rearrange("p (r q) -> p r q", r=n)[:, :, 0:P]
                    pool.affine_select(out=d, in_=d, compare_op=ALU.is_ge, fill=0.0, base=0,
                                       pattern=[[0, n], [1, P]], channel_multiplier=-1).then_inc(masked, 1)

            pool.wait_ge(v_done, 4)
            pool.wait_ge(v_ones, 2)
            load_v(0, 0)
            for b in range(BATCH):
                group(0, b, False)
            with pool.Fori(1, KVH - 1) as i:
                for b in range(BATCH):
                    group(i, b, False)
            for b in range(BATCH):
                group(KVH - 1, b, True)

            divide(KVH - 1, 1, 1)

            pool.wait_ge(z_done, 4 * KVH)
            pool.wait_ge(side_read, SIDE * BATCH * KVH)
            pool.memset(ones_b[:, :], 1.0).then_inc(consts, 1)
            pool.memset(tri[:, :], 1.0).then_inc(consts, 1)
            pool.wait_ge(consts, 2)
            pool.affine_select(out=tri[:, :], in_=tri[:, :], compare_op=ALU.is_gt, fill=0.0, base=0,
                               pattern=[[1, P]], channel_multiplier=-1).then_inc(consts, 1)
            pool.iota(top8[:, 0:8, :].rearrange("p a b -> p (a b)").bitcast(U32), pattern=[[1, E]], base=0,
                      channel_multiplier=0).then_inc(consts, 1)
            for h in range(2):
                pool.iota(top8[:, 8 + h, :].bitcast(U32), pattern=[[LANE_TILES, LANES]], base=-h,
                          channel_multiplier=1).then_inc(consts, 1)
            pool.iota(idxf[:, 0:4, :].rearrange("p a b -> p (a b)").bitcast(U32), pattern=[[SUB, NTOK // SUB]], base=0,
                      channel_multiplier=0).then_inc(consts, 1)
            pool.iota(token_ids[:, :], pattern=[[P, NT]], base=0, channel_multiplier=1).then_inc(consts, 1)
            pool.memset(tab[:, :], 0).then_inc(consts, 1)
            pool.wait_ge(consts, 9)
            pool.tensor_copy(iota_e[:, :], top8[:, 0:8, :].rearrange("p a b -> p (a b)").bitcast(U32))\
                .then_inc(consts, 1)
            pool.tensor_copy(tile_no[:, :], top8[:, 8:10, :].rearrange("p a b -> p (a b)").bitcast(U32))\
                .then_inc(consts, 1)
            pool.tensor_copy(iota_c[:, :], idxf[:, 0:4, :].rearrange("p a b -> p (a b)").bitcast(U32))\
                .then_inc(consts, 1)
            pool.wait_ge(consts, 12)
            pool.affine_select(out=tile_no[:, LANES:], in_=tile_no[:, LANES:], compare_op=ALU.is_gt, fill=-1.0, base=0,
                               pattern=[[0, LANES]], channel_multiplier=1).then_inc(consts, 1)
            pool.dma_start(slot_tokens.rearrange("(s p) o -> s (p o)", p=P), tab[0:PAIRS, :]).then_inc(table_zero, 16)
            pool.wait_ge(table_zero, 16)
            for n in range(HC):
                pool.wait_ge(silu_done, n + 1)
                pool.wait_ge(up_copied, n + 1)
                pool.tensor_tensor(hidden[:, n, :], silu_s[:, n % 2, :], up_s[:, n % 2, :], ALU.mult)\
                    .then_inc(hidden_done, 1)
            pool.wait_ge(slots_ready, 1)
            for k in range(TOPK):
                for t in range(NT):
                    pool.indirect_dma_start(out=slot_tokens[:, :],
                                            out_offset=bass.IndirectOffsetOnAxis(ap=slot_u[:, k, t:t + 1], axis=0),
                                            in_=token_ids[:, t:t + 1], in_offset=None).then_inc(table_set, 16)

            def gather_tokens(i, j):
                n = JP * i + j
                wait(pool, xg_turned, n - 3)
                pool.tensor_copy(idx[:, j:j + 1], tab_t[:, bass.ds(j * LANE_TILES + i, 1)]).then_inc(idx_set, 1)
                wait_alone(pool, idx_set, n + 1, pool_passed)
                pool.indirect_dma_start(out=xg[:, j, :], out_offset=None, in_=xn2_rows[:, :],
                                        in_offset=bass.IndirectOffsetOnAxis(ap=idx[:, j:j + 1], axis=0))\
                    .then_inc(xg_in[j], 16)

            pool.wait_ge(table_ready, 1)
            pool.wait_ge(xn2_stored, 16 * NT)
            for j in range(JP):
                gather_tokens(0, j)
            with pool.Fori(1, LANE_TILES) as i:
                for j in range(JP):
                    gather_tokens(i, j)
            for s in yb_stored:
                pool.wait_ge(s, 16 * PAIRS)
            for t in range(NT):
                if t >= YK:
                    pool.wait_ge(mixed, TOPK * (t - YK + 1))
                for k in range(TOPK):
                    pool.indirect_dma_start(out=yk[:, t % YK, k, :], out_offset=None, in_=slot_y[:, :],
                                            in_offset=bass.IndirectOffsetOnAxis(ap=slot_u[:, k, t:t + 1], axis=0))\
                        .then_inc(yk_in[t % YK], 16)

        @block.scalar
        def _(act):
            for dst, src in ((wk_s, wk), (wv_s, wv), (wq_s, wq), (wo_s, wo)):
                if dst is not wo_s:
                    act.dma_start(dst[:, :, :], src.rearrange("(c p) n -> p c n", p=P)).then_inc(w_in, 16)
            wo_rows = wo.rearrange("(c k r d) n -> r k d c n", k=2, r=REP, d=HD)
            for r in range(REP):
                for k in range(2):
                    at = (2 * r + k) * HD
                    act.dma_start(wo_s[at:at + HD, :, :], wo_rows[r, k]).then_inc(w_in, 16)
            act.dma_start(router_s[:, :, :], router_w.rearrange("(c p) e -> p c e", p=P)).then_inc(w_in, 16)
            act.dma_start(bias_s[:, :], router_bias.partition_broadcast(P)).then_inc(w_in, 16)
            act.wait_ge(eps_set, 1)

            def deviation(g):
                act.wait_ge(ln_aggr, g + 1)
                act.activation(std[:, 4 * g:4 * g + 4], mv[:, 4 * g:4 * g + 4, 1], ACT.Sqrt, bias=eps_s[:, :])\
                   .then_inc(ln_std, 1)

            deviation(0)
            qk = 0
            for j, (kind, a) in enumerate(jobs):
                if kind == "T" and a % 4 == 0 and a + 4 < NT:
                    deviation(a // 4 + 1)
                if kind == "T" and a % 2 == 1:
                    act.wait_ge(prep_done, j + 1)
                    act.activation(XT[:, :, a * P:(a + 1) * P], bank(banks[j]).rearrange("p (c t) -> p c t", c=C),
                                   ACT.Copy).then_inc(xt_ready[1], 1)
                if kind == "QK":
                    act.wait_ge(prep_done, j + 1)
                    if qk >= 2:
                        act.wait_ge(parts_out[qk % 2], 16 * (qk // 2))
                    act.activation(stage[:, qk % 2, 0, :], bank(banks[j]), ACT.Copy).then_inc(part_hi, 1)
                    act.wait_ge(part_rest, qk + 1)
                    act.activation(stage[:, qk % 2, 1, :], rest[:, :], ACT.Copy).then_inc(part_mid, 1)
                    qk += 1

            def exps(i):
                for n0 in range(BATCH * NS):
                    n = BATCH * NS * i + n0
                    act.wait_ge(scores_done, n + 1)
                    wait(act, pv_done, n - 3)
                    act.activation(probs[:, n0 % 4, :], PS[:, (n0 % 2) * 2 * BANK:(n0 % 2 + 1) * 2 * BANK], ACT.Exp,
                                   scale=HD ** -0.5).then_inc(exp_done, 1)

            exps(0)
            with act.Fori(1, KVH - 1) as i:
                exps(i)
            exps(KVH - 1)

            for g in range(4):
                act.wait_ge(ln2_aggr, g + 1)
                act.activation(std[:, 4 * g:4 * g + 4], mv[:, 4 * g:4 * g + 4, 1], ACT.Sqrt, bias=eps_s[:, :])\
                   .then_inc(ln2_std, 1)
                act.wait_ge(stage_in[g % 2], 16 * (g // 2 + 1))
                act.activation(shared_w[:, 2 * (g // 2), (g % 2) * C:(g % 2 + 1) * C, :],
                               w_stage[:, g % 2, :].rearrange("p (c n) -> p c n", c=C), ACT.Copy, scale=W_SCALE)\
                   .then_inc(w_hi_ready, 1)
                for t in range(4 * g, 4 * g + 4):
                    act.wait_ge(turn2_done, t + 1)
                    if t >= 4:
                        act.wait_ge(logits_done, t - 3)
                        act.wait_ge(x_lo_ready, t - 3)
                    src = bank(4 + t % 2).rearrange("p (c t) -> p c t", c=C)
                    act.activation(x_turned[:, t % 4, :, :], src, ACT.Copy).then_inc(xt2_ready, 1)
                    act.activation(x_hi[:, :, t * P:(t + 1) * P], src, ACT.Copy, scale=X_SCALE).then_inc(x_hi_ready, 1)
            act.wait_ge(route, 2)
            act.activation(ex[:, :, :], tmp[:, :, :], ACT.Exp).then_inc(ex_ready, 1)
            def shared_silu(g):
                for n in range(HC * g, HC * (g + 1)):
                    act.wait_ge(up_done, n + 1)
                    if n >= 2:
                        act.wait_ge(hidden_done, n - 1)
                    act.activation(silu_s[:, n % 2, :], bank(2 * (n % 2)), ACT.Silu,
                                   scale=1 / (X_SCALE * W_SCALE)).then_inc(silu_done, 1)
                    if g == 0:
                        act.activation(up_s[:, n % 2, :], bank(2 * (n % 2) + 1), ACT.Copy,
                                       scale=1 / (X_SCALE * W_SCALE)).then_inc(up_copied, 1)

            for g in range(EARLY):
                shared_silu(g)

            def turned_tokens(n, k):
                act.wait_ge(xg_turned, n + 1)
                wait(act, e_up, n - 1)
                act.activation(xgt[:, k % 2, :], bank(k % 2), ACT.Copy).then_inc(xgt_ready, 1)

            def silu(n, k):
                act.wait_ge(e_up, n + 1)
                wait(act, e_hidden, n - 1)
                act.activation(sg[:, k % 2, :], bank(2 + k % 2, F), ACT.Silu).then_inc(e_silu, 1)

            def store_y(i, j):
                act.wait_ge(yb_ready, JP * i + j + 1)
                rows = slot_y.rearrange("(j l i q) d -> j l i q d", l=2, i=LANE_TILES, q=SUB)
                for l in range(2):
                    act.dma_start(rows[j, l, bass.ds(i, 1), :, :].rearrange("o q d -> (o q) d"),
                                  yb[l * SUB:(l + 1) * SUB, j % 2, :]).then_inc(yb_stored[j % 2], 16)

            def expert_pairs(i, first, last):
                for j in range(JP):
                    n = JP * i + j
                    if not (last and j == JP - 1):
                        turned_tokens(n + 1, j + 1)
                    silu(n, j)
                    if not (first and j < 3):
                        store_y(i if j == 3 else i - 1, (j + 1) % JP if j < 3 else 0)

            turned_tokens(0, 0)
            expert_pairs(0, True, False)
            with act.Fori(1, LANE_TILES - 1) as i:
                expert_pairs(i, False, False)
            expert_pairs(LANE_TILES - 1, False, True)
            for j in range(1, JP):
                store_y(LANE_TILES - 1, j)
            act.wait_ge(e_down, PAIRS)
            act.wait_ge(e_hidden, PAIRS)
            for g in range(EARLY, 4):
                shared_silu(g)
            for s in yb_stored:
                act.wait_ge(s, 16 * PAIRS)

        @block.tensor
        def _(pe):
            def piece(b, k, index, at, before):
                wait(pe, side_read, index + 1 - before)
                qt, lo, n = PIECES[k % len(PIECES)]
                pe.matmul(bank(at, n), q_max[b][0:STACK, k // len(PIECES), qt * P:(qt + 1) * P],
                          k_max[b][0:STACK, lo:lo + n], start=True, stop=True).then_inc(side_done, 1)

            def turn(g, b, index, at, before):
                pe.wait_ge(max_ready, g + 1)
                wait(pe, side_read, index + 1 - before)
                pe.transpose(bank(at, P)[0:REP * QT, :], maxes[b][:, :, :].rearrange("p r t -> p (r t)"),
                             ident[:, :]).then_inc(side_done, 1)

            def side(index, at, before, group, k):
                i, b = group
                if k == 0:
                    pe.wait_ge(max_in[b], 16 * 2 * len(Q_PART) * (i + 1))
                if k is None:
                    turn(BATCH * i + b, b, index, at, before)
                else:
                    piece(b, k, index, at, before)

            def job_read(j):
                kind, a = jobs[j]
                if kind == "T":
                    pe.wait_ge(xt_ready[a % 2], a // 2 + 1)
                elif kind == "QK":
                    pe.wait_ge(part_rest, 1 + sum(k == "QK" for k, _ in jobs[:j]))
                else:
                    pe.wait_ge(v_done, a + 1)

            def inner_item(j, k):
                if k < len(inner[j]):
                    item = inner[j][k]
                    if item[0] < 2:
                        job_read(side_user[item[0]])
                    side(*item)

            pe.wait_ge(ident_set, 1)
            for j, (kind, a) in enumerate(jobs):
                if bank_user[j] is not None:
                    job_read(bank_user[j])
                if kind == "T":
                    pe.wait_ge(xn_ready, a + 1)
                    for c in range(C):
                        mm = pe.transpose(PS[:, banks[j] * BANK + c * P:banks[j] * BANK + (c + 1) * P],
                                          XN[:, a, c * P:(c + 1) * P], ident[:, :])
                elif kind == "QK":
                    m, g = a
                    if m == 0:
                        pe.wait_ge(w_in, 16 * 13)
                        for s in xt_ready:
                            pe.wait_ge(s, 2 * g + 2)
                    for c in range(C):
                        w = wq_s[:, c, m * P:(m + 1) * P] if m < C else wk_s[:, c, :]
                        mm = pe.matmul(bank(banks[j]), w, XT[:, c, g * BANK:(g + 1) * BANK],
                                       start=(c == 0), stop=(c == C - 1))
                        inner_item(j, c)
                else:
                    for t in range(4):
                        for c in range(C):
                            mm = pe.matmul(PS[:, banks[j] * BANK + t * P:banks[j] * BANK + (t + 1) * P],
                                           XT[:, c, (4 * a + t) * P:(4 * a + t + 1) * P], wv_s[:, c, :],
                                           start=(c == 0), stop=(c == C - 1))
                        inner_item(j, t)
                mm.then_inc(prep_done, 1)

            def scores(i, b, s, between=()):
                n, parity = NS * (BATCH * i + b) + s, (NS * b + s) % 2
                if s == 0:
                    pe.wait_ge(exp_in[b], 16 * 2 * len(Q_PART) * (i + 1))
                    pe.wait_ge(rows_in, 32 * (BATCH * i + b + 1))
                wait(pe, exp_done, n - 1)
                for kt, q0, qn, col in STEPS[s]:
                    rows = BANK // qn
                    for r in range(0, REP, rows):
                        if (kt, r) != (STEPS[s][0][0], 0):
                            for item in between:
                                side(*item)
                        at = parity * 2 * BANK + col + r * qn
                        mm = pe.matmul(PS[:, at:at + BANK], k_exp[b][0:KROWS, kt * P:(kt + 1) * P],
                                       q_exp[b][0:KROWS, r:r + rows, q0:q0 + qn], start=True, stop=True)
                mm.then_inc(scores_done, 1)

            def values(i, b, s, last):
                g = BATCH * i + b
                n = NS * g + s
                pe.wait_ge(exp_done, n + 1)
                if s == 0:
                    pe.wait_ge(v_in[b], i + 1)
                    wait(pe, turn_done, 2 * g - 1)
                    if last and b == 1:
                        pe.wait_ge(side_read, SIDE * BATCH * KVH)
                    elif not (isinstance(i, int) and i == 0 and b == 0):
                        pe.wait_ge(side_read, SIDE * g + LAST_IN[0])
                if s == NS0:
                    wait(pe, turn_done, 2 * g)
                    if not (last and b == 1):
                        pe.wait_ge(side_read, SIDE * (g + 1) + LAST_IN[1])
                if STEPS[s][0][1] == STEPS[s][0][0] * P:
                    pe.wait_ge(masked, MASKS * g + sum(x[0][1] == x[0][0] * P for x in STEPS[:s + 1]))
                for kt, q0, qn, col in STEPS[s]:
                    for r in range(REP):
                        at = 6 * BANK + q0
                        a = col + r * qn
                        mm = pe.matmul(PS[32 * r:32 * r + 32, at:at + qn], v_head[b][:, kt, :],
                                       probs[:, (NS * b + s) % 4, a:a + qn], start=s in (0, NS0), stop=False,
                                       skip_group_check=True)
                mm.then_inc(pv_done, 1)

            def group(i, b, last):
                for s in range(NS):
                    items = side_items(i, b, last, s)
                    if s == TURN_1 + 1:
                        wait(pe, turn_done, 2 * (BATCH * i + b))
                    if s == TURN_0 + 1:
                        pe.wait_ge(turn_done, 2 * (BATCH * i + b) + 1)
                    for item in items[:1]:
                        side(*item)
                    if s + 1 < NS:
                        scores(i, b, s + 1, items[1:2])
                    elif not (last and b == 1):
                        scores(i + b, 1 - b, 0, items[1:2])
                    for item in items[2:]:
                        side(*item)
                    if s > 0:
                        values(i, b, s - 1, last)
                    elif not (isinstance(i, int) and i == 0 and b == 0):
                        values(i - 1 + b, 1 - b, NS - 1, False)

            pe.wait_ge(k_ones, 2)
            pe.wait_ge(v_done, 4)
            pe.wait_ge(part_rest, QK_JOBS)
            for item in rest_items:
                side(*item)
            scores(0, 0, 0)
            for b in range(BATCH):
                group(0, b, False)
            with pe.Fori(1, KVH - 1) as i:
                for b in range(BATCH):
                    group(i, b, False)
            for b in range(BATCH):
                group(KVH - 1, b, True)
            values(KVH - 1, 1, NS - 1, True)

            def project(t):
                pe.wait_ge(yt_done, C * (t // QT + 1))
                if t == 0:
                    pe.wait_ge(exp_done, NS * BATCH * KVH)
                if t >= 4:
                    pe.wait_ge(x1_done, t - 3)
                for c in range(C):
                    mm = pe.matmul(bank(t % 4), YT[:, c, t * P:(t + 1) * P], wo_s[:, c, :],
                                   start=(c == 0), stop=(c == C - 1))
                mm.then_inc(wo_done, 1)

            def turn_tokens(t):
                pe.wait_ge(xn2_ready, t + 1)
                if t >= 2:
                    pe.wait_ge(x_hi_ready, t - 1)
                for c in range(C):
                    mm = pe.transpose(PS[:, (4 + t % 2) * BANK + c * P:(4 + t % 2) * BANK + (c + 1) * P],
                                      xn2[:, t % 4, c * P:(c + 1) * P], ident[:, :])
                mm.then_inc(turn2_done, 1)

            def logits(t):
                pe.wait_ge(xt2_ready, t + 1)
                at = 6 * BANK + t * E
                for c in range(C):
                    mm = pe.matmul(PS[:, at:at + E], x_turned[:, t % 4, c, :], router_s[:, c, :],
                                   start=(c == 0), stop=(c == C - 1))
                mm.then_inc(logits_done, 1)

            for g in range(5):
                if g < 4:
                    for t in range(4 * g, 4 * g + 4):
                        project(t)
                if g >= 1:
                    for t in range(4 * g - 4, 4 * g):
                        turn_tokens(t)
                    for t in range(4 * g - 4, 4 * g):
                        logits(t)

            def ranks():
                pe.wait_ge(masks_ready, 1)
                for h in range(2):
                    half = slice(h * NT // 2, (h + 1) * NT // 2)
                    flat = lambda v: v[:, half, :].rearrange("p t e -> p (t e)")
                    pe.matmul(bank(6 + h), tri[:, :], flat(mask), start=True, stop=False)
                    pe.matmul(bank(6 + h), ones_b[:, :], flat(cum), start=False, stop=True)
                pe.matmul(bank(4, 1)[0:E, :], total_b[:, :], ones_b[:, 0:1], start=True, stop=True)\
                  .then_inc(ranks_done, 1)

            def starts():
                pe.wait_ge(tiles_ready, 1)
                pe.matmul(bank(5, E), tiles_b[0:E, :], tri[0:E, 0:E], start=True, stop=True).then_inc(starts_done, 1)

            pe.wait_ge(shared_in, 16)
            pe.wait_ge(x1_done, NT)
            pe.wait_ge(w_lo_ready, 4)
            def shared(g):
                pe.wait_ge(x_lo_ready, 4 * (g + 1))
                for hc in range(HC):
                    n = HC * g + hc
                    if n >= 2:
                        pe.wait_ge(hidden_done, n - 1)
                    s, at = hc // C, (hc % C) * P
                    tokens = slice(g * BANK, (g + 1) * BANK)
                    for k in range(2):
                        for c in range(C):
                            for w, v in ((0, x_hi), (0, x_lo), (1, x_hi)):
                                mm = pe.matmul(bank(2 * (n % 2) + k), shared_w[:, 2 * k + w, C * s + c, at:at + P],
                                               v[:, c, tokens], start=(c == 0 and w == 0 and v is x_hi),
                                               stop=(c == C - 1 and w == 1))
                    mm.then_inc(up_done, 1)
                    if g == 0 and hc == RANKS_AT:
                        ranks()
                    if g == 0 and hc == STARTS_AT:
                        starts()
                if g == 0:
                    pe.wait_ge(experts_ready, 1)
                for t in range(4 * g, 4 * g + 4):
                    if t >= 2:
                        pe.wait_ge(shared_added, t - 1)
                    for hc in range(HC):
                        if t == 4 * g:
                            pe.wait_ge(hidden_done, HC * g + hc + 1)
                        mm = pe.matmul(bank(4 + t % 2), hidden[:, hc, (t % 4) * P:(t % 4 + 1) * P], swd_s[:, hc, :],
                                       start=(hc == 0), stop=(hc == HC - 1))
                    mm.then_inc(down_done, 1)
                    if t == TABLE_AT:
                        pe.wait_ge(table_float, 1)
                        pe.transpose(bank(6, PAIRS), tmp[:, 0:2, :].rearrange("p a b -> p (a b)")[0:PAIRS, :],
                                     ident[0:PAIRS, 0:PAIRS]).then_inc(table_turned, 1)

            for g in range(EARLY):
                shared(g)

            def turn_slots(n, k, i):
                j = k % JP
                pe.wait_ge(xg_in[j], 16 * (i + k // JP + 1))
                wait(pe, xgt_ready, n - 1)
                for c in range(C):
                    mm = pe.transpose(PS[:, (k % 2) * BANK + c * P:(k % 2) * BANK + (c + 1) * P],
                                      xg[:, j, c:D:C], ident[:, :])
                mm.then_inc(xg_turned, 1)

            def expert_up(n, j, i):
                for l in range(2):
                    pe.wait_ge(lane_up_in[2 * j + l], 32 * (i + 1))
                pe.wait_ge(xgt_ready, n + 1)
                wait(pe, e_hidden, n - 1)
                for c in range(C):
                    for l in range(2):
                        at = (2 + j % 2) * BANK
                        mm = pe.matmul(PS[l * SUB:(l + 1) * SUB, at:at + 2 * F],
                                       xgt[:, j % 2, c * P + l * SUB:c * P + (l + 1) * SUB],
                                       lane_w[2 * j + l][:, 0:2, c * F:(c + 1) * F], start=(c == 0), stop=(c == C - 1))
                mm.then_inc(e_up, 1)

            def turn_hidden(n, j):
                pe.wait_ge(e_hidden, n + 1)
                wait(pe, e_turned, n - 1)
                pe.transpose(bank(6 + j % 2, P), ht[:, j % 2, :], ident[:, :]).then_inc(e_turn, 1)

            def expert_down(n, j, i):
                for l in range(2):
                    pe.wait_ge(lane_down_in[2 * j + l], 16 * (i + 1))
                pe.wait_ge(e_turned, n + 1)
                wait(pe, yb_ready, n - 1)
                for l in range(2):
                    mm = pe.matmul(PS[l * SUB:(l + 1) * SUB, (4 + j % 2) * BANK:(5 + j % 2) * BANK],
                                   hg[:, j % 2, l * SUB:(l + 1) * SUB], lane_w[2 * j + l][:, 2, :],
                                   start=True, stop=True)
                mm.then_inc(e_down, 1)

            def expert_pairs(i, first, last):
                for j in range(JP):
                    n = JP * i + j
                    if not (last and j == JP - 1):
                        turn_slots(n + 1, j + 1, i)
                    expert_up(n, j, i)
                    if not (first and j < 1):
                        turn_hidden(n - 1, (j - 1) % JP)
                    if not (first and j < 2):
                        expert_down(n - 2, (j - 2) % JP, i if j >= 2 else i - 1)

            pe.wait_ge(table_ready, 1)
            turn_slots(0, 0, 0)
            expert_pairs(0, True, False)
            with pe.Fori(1, LANE_TILES - 1) as i:
                expert_pairs(i, False, False)
            expert_pairs(LANE_TILES - 1, False, True)
            turn_hidden(PAIRS - 1, JP - 1)
            expert_down(PAIRS - 2, JP - 2, LANE_TILES - 1)
            expert_down(PAIRS - 1, JP - 1, LANE_TILES - 1)

            pe.wait_ge(yb_ready, PAIRS)
            for g in range(EARLY, 4):
                shared(g)

        @block.vector
        def _(dve):
            def normalise_group(g):
                dve.wait_ge(x_in[g], 16)
                for t in range(4 * g, 4 * g + 4):
                    last = dve.bn_stats(stats[:, t, :], X[:, t, :])
                last.then_inc(ln_stats, 1)
                dve.wait_ge(ln_stats, g + 1)
                for t in range(4 * g, 4 * g + 4):
                    last = dve.bn_aggr(mv[:, t, :], stats[:, t, :])
                last.then_inc(ln_aggr, 1)
                dve.wait_ge(ln_std, g + 1)
                dve.reciprocal(rstd[:, 4 * g:4 * g + 4], std[:, 4 * g:4 * g + 4]).then_inc(ln_rstd, 1)
                dve.wait_ge(ln_rstd, g + 1)
                for t in range(4 * g, 4 * g + 4):
                    dve.tensor_scalar(XN[:, t, :], X[:, t, :], mv[:, t, 0:1], rstd[:, t:t + 1],
                                      ALU.subtract, ALU.mult).then_inc(xn_ready, 1)

            def reduce_piece(b, k, index, at):
                r = k // len(PIECES)
                qt, lo, n = PIECES[k % len(PIECES)]
                src = bank(at, n)
                if lo + n == (qt + 1) * P:
                    wait_alone(dve, side_done, index + 1, dve_passed)
                    dve.tensor_tensor_reduce(out=junk[:, at - SIDE_BANKS[0], 0:n], in0=src, in1=causal[:, BANK - n:],
                                             scale=1.0, scalar=-3e38, op0=ALU.add, op1=ALU.max,
                                             accum_out=maxes[b][:, r, qt:qt + 1]).then_inc(side_read, 1)
                else:
                    dve.wait_ge(side_done, index + 1)
                    dve.reduce_max(max_low[:, r, qt - QT // 2:qt - QT // 2 + 1], src, AXX).then_inc(side_read, 1)

            def turn_rows(g, index, at):
                dve.wait_ge(side_done, index + 1)
                src = bank(at, P)[0:REP * QT, :]
                dve.tensor_scalar(max_rows[:, 0, :], src, -1.0, None, ALU.mult).then_inc(max_hi, 1)
                dve.wait_ge(max_hi, g + 1)
                dve.scalar_tensor_tensor(out=max_rows[:, 1, :], in0=src, scalar=-1.0, in1=max_rows[:, 0, :],
                                         op0=ALU.mult, op1=ALU.subtract).then_inc(side_read, 1)
                dve.wait_ge(side_read, index + 1)
                dve.sem_inc(rows_ready, 1)

            def side(index, at, before, group, k):
                i, b = group
                if k is None:
                    turn_rows(BATCH * i + b, index, at)
                else:
                    reduce_piece(b, k, index, at)
                if k == SIDE - 2:
                    dve.wait_ge(side_read, index + 1)
                    dve.tensor_tensor(maxes[b][:, :, QT // 2:], maxes[b][:, :, QT // 2:], max_low[:, :, :],
                                      ALU.max).then_inc(max_ready, 1)

            def inner_item(j, k):
                if k < len(inner[j + 1]):
                    side(*inner[j + 1][k])

            normalise_group(0)
            dve.wait_ge(causal_set, 1)
            qk = 0
            for j, (kind, a) in enumerate(jobs):
                if kind == "T" and a % 4 == 0 and a // 4 + 1 < 4:
                    normalise_group(a // 4 + 1)
                if kind == "T" and a % 2 == 0:
                    dve.wait_ge(prep_done, j + 1)
                    dve.tensor_copy(XT[:, :, a * P:(a + 1) * P], bank(banks[j]).rearrange("p (c t) -> p c t", c=C))\
                       .then_inc(xt_ready[0], 1)
                if kind == "QK":
                    dve.wait_ge(part_hi, qk + 1)
                    dve.tensor_tensor(rest[:, :], bank(banks[j]), stage[:, qk % 2, 0, :], ALU.subtract)\
                       .then_inc(part_rest, 1)
                    inner_item(j, 0)
                    inner_item(j, 1)
                    dve.wait_ge(part_mid, qk + 1)
                    dve.tensor_tensor(stage[:, qk % 2, 2, :], rest[:, :], stage[:, qk % 2, 1, :], ALU.subtract)\
                       .then_inc(part_low, 1)
                    inner_item(j, 2)
                    dve.wait_ge(part_low, qk + 1)
                    inner_item(j, 3)
                    qk += 1
                if kind == "V":
                    dve.wait_ge(prep_done, j + 1)
                    dve.tensor_copy(v_all[:, 4 * a:4 * a + 4, :, :],
                                    bank(banks[j]).rearrange("p (t k d) -> p t k d", t=4, k=KVH)).then_inc(v_done, 1)
                if kind != "QK":
                    for k in range(len(inner[j + 1])):
                        inner_item(j, k)

            def normalise(i, b, half, stage):
                g = BATCH * i + b
                n = 2 * g + half
                t = turned[:, :].rearrange("p (k f) -> p k f", f=32)
                if stage == 0:
                    dve.wait_ge(pv_done, NS * g + (NS if half else NS0))
                    wait(dve, z_done, n)
                    dve.transpose(turned[:, :], bank(6 + half)).then_inc(turn_done, 1)
                if stage == 1:
                    dve.wait_ge(turn_done, n + 1)
                    dve.reciprocal(recip[:, :], t[:, :, HD]).then_inc(recip_done, 1)
            def group(i, b, last):
                for s in range(NS):
                    items = side_items(i, b, last, s)
                    for k in range(max(2, len(items))):
                        if k < len(items):
                            side(*items[k])
                        for first, half in ((TURN_1, 1), (TURN_0, 0)):
                            at = 2 * (s - first) + k
                            if k < 2 and at in (0, 1) and not (half and isinstance(i, int) and i == 0 and b == 0):
                                if half:
                                    normalise(i - 1 + b, 1 - b, half, at)
                                else:
                                    normalise(i, b, half, at)

            for item in rest_items:
                side(*item)
            for b in range(BATCH):
                group(0, b, False)
            with dve.Fori(1, KVH - 1) as i:
                for b in range(BATCH):
                    group(i, b, False)
            for b in range(BATCH):
                group(KVH - 1, b, True)

            def turn_result(b):
                for c in range(C):
                    dve.transpose(YT[:, c, b * SEQ:(b + 1) * SEQ],
                                  Z[:, b, :, 2 * c:2 * c + 2, :].rearrange("p k h e -> p k (h e)")).then_inc(yt_done, 1)

            dve.wait_ge(z_done, 4 * KVH - 2)
            turn_result(0)
            for k in range(2):
                normalise(KVH - 1, 1, 1, k)
            dve.wait_ge(z_done, 4 * KVH)
            turn_result(1)

            def low_parts(g):
                for t in range(4 * g, 4 * g + 4):
                    at = slice(t * P, (t + 1) * P)
                    dve.wait_ge(x_hi_ready, t + 1)
                    dve.scalar_tensor_tensor(out=x_lo[:, :, at], in0=x_turned[:, t % 4, :, :], scalar=X_SCALE,
                                             in1=x_hi[:, :, at], op0=ALU.mult, op1=ALU.subtract)\
                       .then_inc(x_lo_ready, 1)

            dve.wait_ge(yt_done, 2 * C)
            for g in range(4):
                ts = range(4 * g, 4 * g + 4)
                for t in ts:
                    dve.wait_ge(wo_done, t + 1)
                    dve.tensor_tensor(X[:, t, :], X[:, t, :], bank(t % 4), ALU.add).then_inc(x1_done, 1)
                dve.wait_ge(x1_done, 4 * g + 4)
                for t in ts:
                    last = dve.bn_stats(stats[:, t, :], X[:, t, :])
                last.then_inc(ln2_stats, 1)
                dve.wait_ge(ln2_stats, g + 1)
                for t in ts:
                    last = dve.bn_aggr(mv[:, t, :], stats[:, t, :])
                last.then_inc(ln2_aggr, 1)
                dve.wait_ge(ln2_std, g + 1)
                dve.reciprocal(rstd[:, 4 * g:4 * g + 4], std[:, 4 * g:4 * g + 4]).then_inc(ln2_rstd, 1)
                dve.wait_ge(ln2_rstd, g + 1)
                if g:
                    dve.wait_ge(xn2_stored, 64 * g)
                    dve.wait_ge(turn2_done, 4 * g)
                for t in ts:
                    dve.tensor_scalar(xn2[:, t % 4, :], X[:, t, :], mv[:, t, 0:1], rstd[:, t:t + 1],
                                      ALU.subtract, ALU.mult).then_inc(xn2_ready, 1)
                if g:
                    low_parts(g - 1)
                dve.wait_ge(w_hi_ready, g + 1)
                part = slice((g % 2) * C, (g % 2 + 1) * C)
                dve.scalar_tensor_tensor(out=shared_w[:, 2 * (g // 2) + 1, part, :],
                                         in0=w_stage[:, g % 2, :].rearrange("p (c n) -> p c n", c=C), scalar=W_SCALE,
                                         in1=shared_w[:, 2 * (g // 2), part, :], op0=ALU.mult, op1=ALU.subtract)\
                   .then_inc(w_lo_ready, 1)
            low_parts(3)

            steps = [0]

            def step(ins):
                steps[0] += 1
                ins.then_inc(route, 1)
                dve.wait_ge(route, steps[0])

            dve.wait_ge(logits_done, NT)
            dve.wait_ge(consts, 13)
            log = PS[:, 6 * BANK:8 * BANK].rearrange("p (t e) -> p t e", t=NT)
            all_te = [P, NT, E]
            step(dve.tensor_reduce(lmax[:, :], log, AXX, ALU.max))
            step(dve.tensor_tensor(tmp[:, :, :], log, lmax[:, :].unsqueeze(2).to_broadcast(all_te), ALU.subtract))
            step(dve.tensor_tensor(biased[:, :, :], log, bias_s[:, :].unsqueeze(1).to_broadcast(all_te), ALU.add))
            for t in range(NT):
                last = dve.max(top8[:, t, :], biased[:, t, :])
            step(last)
            for t in range(NT):
                last = dve.max_index(idx8[:, t, :], top8[:, t, :], biased[:, t, :])
            step(last)
            step(dve.tensor_copy(idxf[:, :, :], idx8[:, :, :]))
            dve.wait_ge(ex_ready, 1)
            for k in range(TOPK):
                step(dve.tensor_tensor(onehot[k][:, :, :], iota_e[:, :].unsqueeze(1).to_broadcast(all_te),
                                       idxf[:, :, k:k + 1].to_broadcast(all_te), ALU.is_equal))
                step(dve.tensor_tensor(tmp[:, :, :], onehot[k][:, :, :], ex[:, :, :], ALU.mult))
                step(dve.tensor_reduce(part_k[:, k, :], tmp[:, :, :], AXX, ALU.add))
                if k == 1:
                    step(dve.tensor_tensor(mask[:, :, :], onehot[0][:, :, :], onehot[1][:, :, :], ALU.add))
                if k > 1:
                    step(dve.tensor_tensor(mask[:, :, :], mask[:, :, :], onehot[k][:, :, :], ALU.add))
            step(dve.memset(cum[:, 0, :], 0.0))
            for t in range(1, NT):
                step(dve.tensor_tensor(cum[:, t, :], cum[:, t - 1, :], mask[:, t - 1, :], ALU.add))
            step(dve.tensor_tensor(total_b[:, :], cum[:, NT - 1, :], mask[:, NT - 1, :], ALU.add))
            dve.sem_inc(masks_ready, 1)
            step(dve.tensor_tensor(lmax[:, :], part_k[:, 0, :], part_k[:, 1, :], ALU.add))
            for k in range(2, TOPK):
                step(dve.tensor_tensor(lmax[:, :], lmax[:, :], part_k[:, k, :], ALU.add))
            step(dve.reciprocal(lmax[:, :], lmax[:, :]))
            step(dve.tensor_tensor(gates[:, :, :], part_k[:, :, :], lmax[:, :].unsqueeze(1).to_broadcast([P, TOPK, NT]),
                                   ALU.mult))
            dve.wait_ge(ranks_done, 1)
            step(dve.tensor_copy(counts[0:E, 0:1], bank(4, 1)[0:E, :]))
            step(dve.tensor_scalar(idxf[0:E, 0:4, :].rearrange("p a b -> p (a b)"), iota_c[0:E, :], counts[0:E, 0:1],
                                   None, ALU.is_lt))
            step(dve.tensor_reduce(counts[0:E, 1:2], idxf[0:E, 0:4, :].rearrange("p a b -> p (a b)"), AXX, ALU.add))
            step(dve.tensor_scalar(tiles_b[0:E, :], ones_b[0:E, :], counts[0:E, 1:2], None, ALU.mult))
            dve.sem_inc(tiles_ready, 1)
            dve.wait_ge(starts_done, 1)
            step(dve.tensor_copy(start_s[:, :], bank(5, E)))
            i24, all_se = slice(0, LANE_TILES), [LANE_TILES, 2 * LANES, E]
            step(dve.tensor_tensor(tmp[i24, :, :], start_s[i24, :].unsqueeze(1).to_broadcast(all_se),
                                   tile_no[i24, :].unsqueeze(2).to_broadcast(all_se), ALU.is_le))
            step(dve.tensor_reduce(found[i24, :], tmp[i24, :, :], AXX, ALU.add))
            step(dve.tensor_tensor(found[i24, LANES:], found[i24, 0:LANES], found[i24, LANES:], ALU.not_equal))
            step(dve.tensor_scalar(found[i24, 0:LANES], found[i24, 0:LANES], -1.0, None, ALU.add))
            step(dve.scalar_tensor_tensor(out=code[i24, :], in0=found[i24, LANES:], scalar=float(E),
                                          in1=found[i24, 0:LANES], op0=ALU.mult, op1=ALU.add))
            dve.sem_inc(experts_ready, 1)
            step(dve.tensor_scalar(start_s[:, :], start_s[:, :], float(SUB), None, ALU.mult))
            step(dve.tensor_tensor(pos[:, :, :], PS[:, 6 * BANK:8 * BANK].rearrange("p (t e) -> p t e", t=NT),
                                   start_s[:, :].unsqueeze(1).to_broadcast(all_te), ALU.add))
            for k in range(TOPK):
                step(dve.tensor_tensor(tmp[:, :, :], onehot[k][:, :, :], pos[:, :, :], ALU.mult))
                step(dve.tensor_reduce(part_k[:, k, :], tmp[:, :, :], AXX, ALU.add))
            step(dve.tensor_copy(slot_u[:, :, :], part_k[:, :, :]))
            dve.sem_inc(slots_ready, 2)

            def shared_hidden(n):
                dve.wait_ge(silu_done, n + 1)
                dve.scalar_tensor_tensor(out=hidden[:, n % HC, :], in0=bank(2 * (n % 2) + 1),
                                         scalar=1 / (X_SCALE * W_SCALE), in1=silu_s[:, n % 2, :],
                                         op0=ALU.mult, op1=ALU.mult).then_inc(hidden_done, 1)

            def shared_add(t):
                dve.wait_ge(down_done, t + 1)
                dve.tensor_tensor(X[:, t, :], X[:, t, :], bank(4 + t % 2), ALU.add).then_inc(shared_added, 1)

            for g in range(EARLY):
                if g:
                    dve.wait_ge(down_done, 4 * g)
                for n in range(HC * g, HC * (g + 1)) if g else ():
                    shared_hidden(n)
                for t in range(4 * g, 4 * g + 4):
                    shared_add(t)
                    if t == TABLE_AT - 1:
                        dve.wait_ge(table_in, 16 * LANES)
                        flat_tmp = tmp[:, 0:2, :].rearrange("p a b -> p (a b)")
                        dve.tensor_copy(flat_tmp[0:PAIRS, :], tab[0:PAIRS, :]).then_inc(table_float, 1)
                        dve.wait_ge(table_turned, 1)
                        dve.tensor_copy(tab_t[:, :], bank(6, PAIRS)).then_inc(table_ready, 1)

            def expert_hidden(n, j):
                dve.wait_ge(e_silu, n + 1)
                wait(dve, e_turn, n - 1)
                at = (2 + j % 2) * BANK + F
                dve.tensor_tensor(ht[:, j % 2, :], sg[:, j % 2, :], PS[:, at:at + F], ALU.mult).then_inc(e_hidden, 1)

            def hidden_turned(n, j):
                dve.wait_ge(e_turn, n + 1)
                wait(dve, e_down, n - 1)
                dve.tensor_copy(hg[:, j % 2, :], bank(6 + j % 2, P)).then_inc(e_turned, 1)

            def expert_y(n, j, count):
                dve.wait_ge(e_down, n + 1)
                wait(dve, yb_stored[j % 2], 32 * count)
                dve.tensor_copy(yb[:, j % 2, :], bank(4 + j % 2)).then_inc(yb_ready, 1)

            def expert_pairs(i, first, last):
                for j in range(JP):
                    n = JP * i + j
                    expert_hidden(n, j)
                    if not (first and j < 1):
                        hidden_turned(n - 1, (j - 1) % JP)
                    if not (first and j < 2):
                        expert_y(n - 2, (j - 2) % JP, 2 * i + (j - 2) // 2)

            expert_pairs(0, True, False)
            with dve.Fori(1, LANE_TILES - 1) as i:
                expert_pairs(i, False, False)
            expert_pairs(LANE_TILES - 1, False, True)
            hidden_turned(PAIRS - 1, JP - 1)
            expert_y(PAIRS - 2, JP - 2, PAIRS // 2 - 1)
            expert_y(PAIRS - 1, JP - 1, PAIRS // 2 - 1)

            def mix(t):
                dve.wait_ge(yk_in[t % YK], 16 * TOPK * (t // YK + 1))
                for k in range(TOPK):
                    if k:
                        dve.wait_ge(mixed, TOPK * t + k)
                    elif t < NT - 4:
                        dve.wait_ge(shared_added, t + 1)
                    dve.scalar_tensor_tensor(out=X[:, t, :], in0=yk[:, t % YK, k, :], scalar=gates[:, k, t:t + 1],
                                             in1=X[:, t, :], op0=ALU.mult, op1=ALU.add).then_inc(mixed, 1)

            for n in range(HC * EARLY, HC * 4):
                if n % HC == 0:
                    dve.wait_ge(down_done, 4 * (n // HC))
                    dve.wait_ge(e_down, PAIRS)
                shared_hidden(n)
                mix(n - HC * EARLY)
                if n % HC == HC - 1:
                    for t in range(4 * (n // HC), 4 * (n // HC) + 4):
                        if t >= NT - 4:
                            dve.wait_ge(mixed, TOPK * (t + 1))
                        shared_add(t)


_INS = ['L0_attn_x', 'L0_attn_wq', 'L0_attn_wk', 'L0_attn_wv', 'L0_attn_wo', 'L0_ffn_router_w', 'L0_ffn_router_bias',
        'L0_ffn_wg', 'L0_ffn_wu', 'L0_ffn_wd', 'L0_ffn_swg', 'L0_ffn_swu', 'L0_ffn_swd']
_OUTS = [((BATCH, SEQ, D), 'float32')]


def kernel(**inputs):
    import numpy as _np
    import concourse.bacc as _bacc
    from concourse import mybir as _mybir
    from concourse.bass_utils import run_bass_kernel_spmd as _run

    nc = _bacc.Bacc("TRN2", target_bir_lowering=False, num_devices=1)
    arrays, args = {}, []
    for name in _INS:
        a = _np.ascontiguousarray(inputs[name])
        arrays[f"in_{name}_dram"] = a
        args.append(nc.dram_tensor(f"in_{name}_dram", a.shape, _mybir.dt.from_np(a.dtype), kind="ExternalInput").ap())
    for i, (shape, dtype) in enumerate(_OUTS):
        dt = _mybir.dt.from_np(_np.dtype(dtype))
        args.append(nc.dram_tensor(f"out_{i}_dram", shape, dt, kind="ExternalOutput").ap())
    build_block(nc, *args)
    r = _run(nc, [arrays], core_ids=[0])
    return r.results[0]["out_0_dram"]
```
